# Optimizing a Trainium2 kernel written in Bass

```python
import numpy as np
import jax
import jax.numpy as jnp

def _softmax(x, axis=-1):
    return jax.nn.softmax(x, axis=axis)

def _gelu(x):
    return jax.nn.gelu(x, approximate=True)

def _silu(x):
    return jax.nn.silu(x)

def _sigmoid(x):
    return jax.nn.sigmoid(x)

def _layernorm(x, axis=-1, eps=1e-05):
    m = jnp.mean(x, axis=axis, keepdims=True)
    v = jnp.var(x, axis=axis, keepdims=True)
    return (x - m) / jnp.sqrt(v + eps)

def _scatter_add(tgt, idx, src, axis=0):
    return tgt.at[idx].add(src)

def _segment_sum(src, seg, n):
    return jax.ops.segment_sum(src, seg, n)
kernel_name = 'mk_seq_postln_d1_jaxref_r4_f4245a'

def setup_inputs(seed: int=0):
    np.random.seed(seed)
    _w = jnp.asarray

    def _L0_attn_setup():
        import jax, jax.numpy as jnp
        import numpy as np
        HIDDEN = 1024
        NUM_HEADS = 32
        HEAD_DIM = HIDDEN // NUM_HEADS
        B, S = (2, 256)

        def _alibi_slopes(n):
            start = 2.0 ** (-2.0 ** (-(np.log2(n) - 3)))
            return np.array([start ** (i + 1) for i in range(n)], dtype=np.float32)
        key = jax.random.key(seed)
        k1, k2, k3, k4 = jax.random.split(key, 4)
        hidden_states = jax.random.normal(k1, (B, S, HIDDEN), jnp.float32)
        Wq = jax.random.normal(k2, (HIDDEN, HIDDEN), jnp.float32) * 0.02
        Wkv = jax.random.normal(k3, (HIDDEN, 2 * HEAD_DIM), jnp.float32) * 0.02
        Wo = jax.random.normal(k4, (HIDDEN, HIDDEN), jnp.float32) * 0.02
        return {'hidden_states': hidden_states, 'Wq': Wq, 'Wkv': Wkv, 'Wo': Wo}
    _L0_attn_in = _L0_attn_setup()

    def _L0_ffn_setup():
        import jax, jax.numpy as jnp
        import numpy as np
        RANKS = (8, 16, 32, 64)
        TOPK = 1
        SCALING = 1.0 / 4
        key = jax.random.key(seed)
        ks = jax.random.split(key, 7)
        D_IN, D_OUT, MAX_R, N_RANKS = (1024, 1024, 64, len(RANKS))
        B_, S_ = (4, 512)
        return {'hidden_states': jax.random.normal(ks[0], (B_, S_, D_IN), jnp.float32), 'W': jax.random.normal(ks[1], (D_OUT, D_IN), jnp.float32) * 0.02, 'b': jax.random.normal(ks[2], (D_OUT,), jnp.float32) * 0.02, 'A': jax.random.normal(ks[3], (MAX_R, D_IN), jnp.float32) * 0.02, 'B': jnp.zeros((D_OUT, MAX_R), jnp.float32) + jax.random.normal(ks[4], (D_OUT, MAX_R), jnp.float32) * 0.02, 'gate_w': jax.random.normal(ks[5], (N_RANKS, D_IN), jnp.float32) * 0.02, 'gate_b': jax.random.normal(ks[6], (N_RANKS,), jnp.float32) * 0.02}
    _L0_ffn_in = _L0_ffn_setup()
    _d = {'L0_attn_hidden_states': _L0_attn_in['hidden_states'], 'L0_attn_Wq': _L0_attn_in['Wq'], 'L0_attn_Wkv': _L0_attn_in['Wkv'], 'L0_attn_Wo': _L0_attn_in['Wo'], 'L0_ffn_W': _L0_ffn_in['W'], 'L0_ffn_b': _L0_ffn_in['b'], 'L0_ffn_A': _L0_ffn_in['A'], 'L0_ffn_B': _L0_ffn_in['B'], 'L0_ffn_gate_w': _L0_ffn_in['gate_w'], 'L0_ffn_gate_b': _L0_ffn_in['gate_b']}
    _x0 = _d['L0_attn_hidden_states']
    _d['L0_attn_hidden_states'] = jax.random.normal(jax.random.fold_in(jax.random.key(seed), 1), (2, 2048, 1024), dtype=_x0.dtype)
    del _x0
    return _d

def reference(L0_attn_hidden_states, L0_attn_Wq, L0_attn_Wkv, L0_attn_Wo, L0_ffn_W, L0_ffn_b, L0_ffn_A, L0_ffn_B, L0_ffn_gate_w, L0_ffn_gate_b):

    def _L0_attn_ref(hidden_states, Wq, Wkv, Wo):
        import jax, jax.numpy as jnp
        import numpy as np
        HIDDEN = 1024
        NUM_HEADS = 32
        HEAD_DIM = HIDDEN // NUM_HEADS
        B, S = (2, 256)

        def _alibi_slopes(n):
            start = 2.0 ** (-2.0 ** (-(np.log2(n) - 3)))
            return np.array([start ** (i + 1) for i in range(n)], dtype=np.float32)
        b, s, h = hidden_states.shape
        scale = HEAD_DIM ** (-0.5)
        q = (hidden_states @ Wq).reshape(b, s, NUM_HEADS, HEAD_DIM)
        kv = hidden_states @ Wkv
        k, v = (kv[..., :HEAD_DIM], kv[..., HEAD_DIM:])
        scores = jnp.einsum('bqhd,bkd->bhqk', q, k) * scale
        pos = jnp.arange(s)
        slopes = jnp.asarray(_alibi_slopes(NUM_HEADS))
        bias = slopes[:, None, None] * (pos[None, None, :] - pos[None, :, None]).astype(jnp.float32)
        causal = pos[None, :] <= pos[:, None]
        scores = jnp.where(causal[None, None], scores + bias[None], -jnp.inf)
        attn = jax.nn.softmax(scores, axis=-1)
        out = jnp.einsum('bhqk,bkd->bqhd', attn, v).reshape(b, s, h)
        return out @ Wo

    def _L0_ffn_ref(hidden_states, W, b, A, B, gate_w, gate_b):
        import jax, jax.numpy as jnp
        import numpy as np
        RANKS = (8, 16, 32, 64)
        TOPK = 1
        SCALING = 1.0 / 4
        bsz, seq, d_in = hidden_states.shape
        out = jnp.einsum('bsd,od->bso', hidden_states, W) + b
        x = hidden_states.reshape(-1, d_in)
        scores = x @ gate_w.T + gate_b
        probs = jax.nn.softmax(scores, axis=-1)
        routing_weights, selected = jax.lax.top_k(probs, TOPK)
        routing_weights = routing_weights / jnp.sum(routing_weights, axis=-1, keepdims=True)
        lora_outputs = jnp.stack([x @ A[:r, :].T @ B[:, :r].T for r in RANKS], axis=1)
        sel = jnp.take_along_axis(lora_outputs, selected[:, :, None], axis=1)
        final = jnp.sum(sel * routing_weights[:, :, None], axis=1)
        return out + final.reshape(bsz, seq, -1)
    x = L0_attn_hidden_states
    x = _layernorm(x + _L0_attn_ref(x, L0_attn_Wq, L0_attn_Wkv, L0_attn_Wo), axis=-1)
    x = _layernorm(x + _L0_ffn_ref(x, L0_ffn_W, L0_ffn_b, L0_ffn_A, L0_ffn_B, L0_ffn_gate_w, L0_ffn_gate_b), axis=-1)
    return x

_drawn_inputs = setup_inputs


def setup_inputs(seed=0):
    import zlib

    import numpy as np

    out = dict(_drawn_inputs(seed))
    spreads = {}
    factors = {'L0_ffn_b': 3.406, 'L0_ffn_gate_b': 23.337}
    for name, (base, spread) in spreads.items():
        noise = np.random.default_rng([zlib.crc32(name.encode()), seed]).standard_normal(out[name].shape)
        drawn = base * np.exp(spread * noise) if base else spread * noise
        out[name] = jnp.asarray(drawn.astype(out[name].dtype))
    for name, factor in factors.items():
        out[name] = (out[name] * factor).astype(out[name].dtype)
    return out
```

```python
from contextlib import ExitStack

import numpy as np
import concourse.bass as bass
from concourse import mybir

ALU = mybir.AluOpType
ACT = mybir.ActivationFunctionType
AX = mybir.AxisListType
F32 = mybir.dt.float32
F32R = mybir.dt.float32r
BF16 = mybir.dt.bfloat16
I32 = mybir.dt.int32

P = 128
B, T, D = 2, 2048, 1024
NH, DH = 32, 32
DC = D // P
GH = P // DH
HG = NH // GH
QB = 512
NSEG = T // QB
QT = QB // P
SCALE = DH ** -0.5
EPS = 1e-5
MASKED = -1.0e30
START = 1
KR = 3 * DH + 1
RANKS = (8, 16, 32, 64)
NRK = len(RANKS)
RM = max(RANKS)
WX = D + RM + NRK
WCH = WX // 3
NTT = B * T // P
DIST0 = NSEG * QT - QT



def alibi_slopes(n):
    start = 2.0 ** (-2.0 ** (-(np.log2(n) - 3)))
    return [float(np.float32(start ** (i + 1))) for i in range(n)]


def ktiles(s):
    return QT * (s + 1)


TILES_B = HG * GH * sum(ktiles(s) for s in range(NSEG))
STEPS_B = TILES_B // GH


def tiles_before(s, u):
    return HG * GH * sum(ktiles(x) for x in range(s)) + u * (GH * ktiles(s))


def steps_before(s, u):
    return HG * sum(ktiles(x) for x in range(s)) + u * ktiles(s)


def parity(s, u0, n=3):
    return (HG * s + u0) % n


def parity_of(count):
    return count % 3


def a_chunks(s):
    return [(h, t, c, QB if c < s else (t + 1) * P) for c in range(s + 1) for h in range(GH) for t in range(QT)]


def plan_step(s, has_a, sa, has_q, prep, has_r):
    n = ktiles(s)
    slots = n * GH
    chunks = a_chunks(sa) if has_a else []
    a_slots = slots - 6
    at = {}
    for i, x in enumerate(chunks):
        at.setdefault(i * a_slots // len(chunks), []).append(("A", x))
    if has_a:
        at.setdefault(a_slots, []).append(("C", 0))
    misc = [("X", j) for j in range(DC)] + [("KV", 0), ("VT", 0)] if prep else []
    if has_q:
        misc += [("Q", j) for j in range(DC)] + [("QE", 0), ("WS", 0)]
    for i, x in enumerate(misc):
        at.setdefault(min(a_slots - 1, 1 + i), []).append(x)
    out = []
    recip_at = {2: 0, 4: 1, 6: 2, 8: 3, 9: 4}
    for k in range(n):
        for h in range(GH):
            i = k * GH + h
            out.append(("S", (k, h)))
            if has_r and i in recip_at:
                out.append(("R", recip_at[i]))
            out += at.get(i, [])
            if k and h % 2:
                out.append(("PV" if h == 1 else "SM", k - 1))
    out += [("PV", n - 1), ("SM", n - 1)]
    out.append(("OE", 0))
    return out


def program(nc, x, wq, wkv, wo, w, bias, la, lb, gate_w, gate_b, out):
    nc.disable_value_cache = True
    slopes = alibi_slopes(NH)
    att = nc.dram_tensor("att_scratch", (B * NSEG * HG, QT, P, P), F32, kind="Internal").ap()
    slope_rows = nc.dram_tensor("slope_rows", (NH, QB), F32, kind="Internal").ap()

    xb = x.rearrange("b (s t p) d -> b s p t d", t=QT, p=P)
    xt = x.rearrange("b (i p) d -> (b i) p d", p=P)
    ot = out.rearrange("b (i p) d -> (b i) p d", p=P)
    wq_v = wq.rearrange("(c p) (g m) -> g p c m", p=P, m=P)
    wo_v = wo.rearrange("(c p) n -> c p n", p=P)
    w_v = w.rearrange("(o p) n -> o p n", p=P)

    with ExitStack() as ctx:
        def sem(name):
            return ctx.enter_context(nc.semaphore(name))

        def sb(c, name, shape, dt):
            return c.enter_context(nc.sbuf_tensor(name, shape, dt))

        def pb(c, name, shape, dt=F32):
            return c.enter_context(nc.psum_tensor(name, shape, dt))

        ident = sb(ctx, "ident", [P, P], F32)
        attention(nc, sb, pb, sem, slopes, xb, wq_v, wkv, att, slope_rows, ident)
        feed_forward(nc, sb, pb, sem, xt, ot, wo_v, w_v, bias, la, lb, gate_w, gate_b, att, ident)


def attention(nc, sb, pb, sem, slopes, xb, wq_v, wkv, att, slope_rows, ident):
    with ExitStack() as ctx:
        identb = sb(ctx, "identb", [P, P], BF16)
        maskb = sb(ctx, "maskb", [P, P], BF16)
        maskt = sb(ctx, "maskt", [P, P], BF16)
        ones = sb(ctx, "ones", [P, DH], F32)
        slope = sb(ctx, "slope", [P, NH], F32)
        slope4 = sb(ctx, "slope4", [P, NH, QT], F32)
        dist_i = sb(ctx, "dist_i", [P, DIST0 + QT], I32)
        dist = sb(ctx, "dist", [P, DIST0 + QT], F32)
        alibi = sb(ctx, "alibi", [P, NH, DIST0 + QT], F32)
        slope_row = sb(ctx, "slope_row", [NH, QB], F32R)
        kpos_i = sb(ctx, "kpos_i", [P, T], I32)
        xs = sb(ctx, "xs", [P, QT, D], F32)
        xh = sb(ctx, "xh", [P, DC, QB], F32R)
        xl = sb(ctx, "xl", [P, DC, QB], F32R)
        wkv_raw = sb(ctx, "wkv_raw", [P, DC, 2 * DH], F32)
        wkvh = sb(ctx, "wkvh", [P, DC, P], F32R)
        wkvl = sb(ctx, "wkvl", [P, DC, P], F32R)
        wq_raw = sb(ctx, "wq_raw", [P, DC, P], F32)
        wqh = sb(ctx, "wqh", [P, DC, P], F32R)
        wql = sb(ctx, "wql", [P, DC, P], F32R)
        kmax = sb(ctx, "kmax", [P, T], F32R)
        kexp = sb(ctx, "kexp", [P, T], F32R)
        vt_sb = sb(ctx, "vt_sb", [P, QB], F32)
        val = sb(ctx, "val", [P, T // P, DH], F32)
        qst = [sb(ctx, f"qst{i}", [P, GH, QB], F32R) for i in range(3)]
        mxp = sb(ctx, "mxp", [P, GH * QT, NSEG], F32)
        mx = sb(ctx, "mx", [P, GH * QT], F32)
        shift = sb(ctx, "shift", [P, GH * QT], F32)
        shift_t = sb(ctx, "shift_t", [GH * QT, P], F32R)
        prob = [sb(ctx, f"prob{i}", [P, GH, QB], F32) for i in range(3)]
        o_sb = sb(ctx, "o_sb", [P, QB], F32)
        s_sb = sb(ctx, "s_sb", [P, QB], F32)
        r_sb = sb(ctx, "r_sb", [P, QB], F32)
        at_sb = sb(ctx, "at_sb", [P, QB], F32)

        ps_s = [pb(ctx, f"ps_s{i}", [P, QB]) for i in range(3)]
        ps_a = [pb(ctx, f"ps_a{i}", [P, QB]) for i in range(2)]
        ps_o = pb(ctx, "ps_o", [P, QB])
        ps_sum = pb(ctx, "ps_sum", [P, QB])
        ps_m = pb(ctx, "ps_m", [P, QB])

        counters = []

        def counter(name):
            counters.append(sem(name))
            return counters[-1]

        pool_c = sem("pool_c")
        vec_c = sem("vec_c")
        pe_c = sem("pe_c")
        rows_out = sem("rows_out")
        wkv_in = sem("wkv_in")
        went_on = sem("went_on")
        x_in = counter("x_in")
        wq_in = counter("wq_in")
        xt_ps = counter("xt_ps")
        xh_done = counter("xh_done")
        xl_done = counter("xl_done")
        kv_ps = counter("kv_ps")
        kv_hi = counter("kv_hi")
        kv_lo = counter("kv_lo")
        kv_done = counter("kv_done")
        vt_ps = counter("vt_ps")
        vt_done = counter("vt_done")
        wqh_done = counter("wqh_done")
        wql_done = counter("wql_done")
        q_ps = counter("q_ps")
        qh_done = counter("qh_done")
        ql_done = counter("ql_done")
        slope_in = counter("slope_in")
        again_in = counter("again_in")
        c_max = counter("c_max")
        c_vec = counter("c_vec")
        c_ps = counter("c_ps")
        c_out = counter("c_out")
        c_in = counter("c_in")
        o_copied = counter("o_copied")
        r_done = counter("r_done")
        at_done = counter("at_done")
        at_out = counter("at_out")
        s_full = counter("s_full")
        e_done = counter("e_done")
        a_full = counter("a_full")
        a_done = counter("a_done")
        pv_done = counter("pv_done")
        VEC_C = 2 * NH + 3 + 2 * QT + 8
        UB = NSEG * HG

        def walk(eng, prologue, unit_step, epilogue):
            with eng.Fori(0, B) as b:
                prologue(b)
                for s in range(NSEG):
                    more = s + 1 < NSEG
                    if s == 0:
                        for u in range(HG - 2):
                            unit_step(b, s, u, u, plan_step(s, True, s, True, False, u > 0))
                    else:
                        with eng.Fori(0, 2) as i:
                            for j in range(3):
                                unit_step(b, s, i * 3 + j, j, plan_step(s, True, s, True, False, True))
                    unit_step(b, s, HG - 2, HG - 2, plan_step(s, True, s, more, more, True))
                    unit_step(b, s, HG - 1, HG - 1, plan_step(s, more, s + 1, more, False, True))
                epilogue(b)

        def ahead(s, u, d, const):
            return (s, u + d) if const + d < HG else (s + 1, const + d - HG)

        def unit_no(b, s, u):
            return b * UB + (HG * s) + u

        with nc.Block() as start:
            @start.sync
            def _(sp):
                for c in counters:
                    sp.sem_inc(c, START)

        block = ctx.enter_context(nc.Block())

        @block.sync
        def _(sp):
            sp.dma_start(wkv_raw[:], wkv.rearrange("(c p) m -> p c m", p=P)).then_inc(wkv_in, 16)
            sp.wait_ge(vec_c, 2 * NH + 3 + 2 * QT)
            sp.dma_start(slope_rows, slope_row[:].bitcast(F32)).then_inc(rows_out, 16)
            sp.wait_ge(rows_out, 16)

            def last_row(buf):
                return qst[buf][3 * DH:KR].bitcast(F32)

            def load_x(b, s):
                sp.wait_ge(xt_ps, START + DC * (b * NSEG + s))
                sp.dma_start(xs[:], xb[b, s]).then_inc(x_in, 16)

            def load_wq(number, u):
                sp.wait_ge(wql_done, START + number)
                sp.dma_start(wq_raw[:], wq_v[u]).then_inc(wq_in, 16)

            def put_slopes(b, s, u, buf, old_tiles):
                g = unit_no(b, s, u)
                sp.wait_ge(s_full, START + old_tiles)
                sp.wait_ge(slope_in, START + 16 * g)
                sp.dma_start(last_row(buf), slope_rows[bass.ds(u * GH, GH)].rearrange("(a h) t -> a h t", a=1)).then_inc(slope_in, 16)

            def repeat_q(b, s, u, buf):
                g = unit_no(b, s, u)
                sp.wait_ge(qh_done, START + GH * (g + 1))
                sp.wait_ge(again_in, START + 16 * g)
                sp.dma_start(qst[buf][DH:2 * DH].bitcast(F32), qst[buf][0:DH].bitcast(F32)).then_inc(again_in, 16)

            def put_shift(b, s, u, buf):
                sp.wait_ge(c_out, START + unit_no(b, s, u) + 1)
                sp.dma_start(last_row(buf), shift_t[:].bitcast(F32)).then_inc(c_in, 16)

            def store_before(g):
                sp.wait_ge(at_done, START + g)
                sp.dma_start(att[g - 1].rearrange("t p q -> p t q"),
                             at_sb[:].rearrange("p (t q) -> p t q", t=QT)).then_inc(at_out, 16)

            def prologue(b):
                load_x(b, 0)
                for u in range(2):
                    put_slopes(b, 0, u, u, b * TILES_B)
                    load_wq(b * UB + u + 1, u + 1)
                    repeat_q(b, 0, u, u)
                put_shift(b, 0, 0, 0)

            def step(b, s, u, const, plan):
                if ("QE", 0) in plan:
                    s2, u2 = ahead(s, u, 2, const)
                    old = b * TILES_B + tiles_before(s, u)
                    put_slopes(b, s2, u2, parity(s, const + 2), old)
                    load_wq(unit_no(b, s, u) + 3, (u + 3) % HG)
                if s == 0 and const == 0:
                    load_x(b, 1)
                if const == HG - 1 and s + 2 < NSEG:
                    load_x(b, s + 2)
                for what, arg in plan:
                    if what == "R" and arg == QT:
                        store_before(unit_no(b, s, u))
                    if what == "QE":
                        repeat_q(b, s2, u2, parity(s, const + 2))
                    if what == "C":
                        s1, u1 = ahead(s, u, 1, const)
                        put_shift(b, s1, u1, parity(s, const + 1))

            def epilogue(b):
                store_before(b * UB + UB)

            sp.dma_start(wq_raw[:], wq_v[0]).then_inc(wq_in, 16)
            walk(sp, prologue, step, epilogue)
            sp.wait_ge(wq_in, START + 16 * (B * UB + 1))
            sp.wait_ge(at_out, START + 16 * B * UB)

        @block.gpsimd
        def _(pool):
            nc.gpsimd.memset(ident[:], 0.0).then_inc(pool_c, 1)
            nc.gpsimd.memset(identb[:], 0.0).then_inc(pool_c, 1)
            nc.gpsimd.memset(maskb[:], 0.0).then_inc(pool_c, 1)
            nc.gpsimd.memset(maskt[:], 0.0).then_inc(pool_c, 1)
            nc.gpsimd.memset(ones[:], 1.0).then_inc(pool_c, 1)
            nc.gpsimd.iota(dist_i[:], [[P, DIST0 + QT]], base=-P * DIST0, channel_multiplier=1).then_inc(pool_c, 1)
            pool.wait_ge(pool_c, 6)
            nc.gpsimd.iota(kpos_i[3 * DH:KR], [[1, T]], base=0, channel_multiplier=0).then_inc(pool_c, 1)
            pool.wait_ge(pool_c, 7)
            for m in (ident, identb):
                nc.gpsimd.affine_select(out=m[:], in_=m[:], compare_op=ALU.not_equal, fill=1.0, base=0,
                                        pattern=[[-1, P]], channel_multiplier=1).then_inc(pool_c, 1)
            nc.gpsimd.affine_select(out=maskb[:], in_=maskb[:], compare_op=ALU.is_ge, fill=MASKED, base=0,
                                    pattern=[[-1, P]], channel_multiplier=1).then_inc(pool_c, 1)
            nc.gpsimd.affine_select(out=maskt[:], in_=maskt[:], compare_op=ALU.is_ge, fill=MASKED, base=0,
                                    pattern=[[1, P]], channel_multiplier=-1).then_inc(pool_c, 1)

            def split_wq(number):
                pool.wait_ge(wqh_done, START + number + 1)
                nc.gpsimd.tensor_tensor(wql[:], wq_raw[:], wqh[:].bitcast(F32), ALU.subtract).then_inc(wql_done, 1)

            def prologue(b):
                for u in range(2):
                    split_wq(b * UB + u + 1)

            def step(b, s, u, const, plan):
                for what, arg in plan:
                    if what == "WS":
                        split_wq(unit_no(b, s, u) + 3)

            split_wq(0)
            walk(pool, prologue, step, lambda b: None)

        @block.scalar
        def _(act):
            def split_x(b, s, j):
                n = DC * (b * NSEG + s) + j
                act.wait_ge(xt_ps, START + n + 1)
                nc.scalar.activation(xh[:, j], ps_m[:], ACT.Copy).then_inc(xh_done, 1)

            def split_wq(number):
                act.wait_ge(wq_in, START + 16 * (number + 1))
                act.wait_ge(q_ps, START + number)
                nc.scalar.activation(wqh[:], wq_raw[:], ACT.Copy).then_inc(wqh_done, 1)

            def take_q(b, s, u, buf, old_tiles):
                act.wait_ge(q_ps, START + unit_no(b, s, u) + 1)
                act.wait_ge(s_full, START + old_tiles)
                for h in range(GH):
                    nc.scalar.activation(qst[buf][0:DH, h], ps_m[h * DH:(h + 1) * DH], ACT.Copy,
                                         scale=SCALE).then_inc(qh_done, 1)

            def prologue(b):
                for j in range(DC):
                    split_x(b, 0, j)
                for u in range(2):
                    take_q(b, 0, u, u, b * TILES_B)
                    split_wq(b * UB + u + 1)

            def step(b, s, u, const, plan):
                g = unit_no(b, s, u)
                for what, arg in plan:
                    if what == "X":
                        split_x(b, s + 1, arg)
                    if what == "WS":
                        split_wq(g + 3)
                    if what == "QE":
                        take_q(b, *ahead(s, u, 2, const), parity(s, const + 2), b * TILES_B + tiles_before(s, u))
                    if what == "S":
                        k, h = arg
                        c0 = max(0, k - QT * s) * P
                        slot = parity_of(steps_before(s, const) + k)
                        bank = parity_of(tiles_before(s, const) + GH * k + h)
                        act.wait_ge(s_full, START + b * TILES_B + tiles_before(s, u) + GH * k + h + 1)
                        if h == 0:
                            early = s == 0 and const == 0 and k < 3
                            act.wait_ge(pv_done, START + b * STEPS_B + (0 if early else steps_before(s, u) + k - 2))
                        nc.scalar.activation(prob[slot][:, h, c0:], ps_s[bank][:, c0:], ACT.Exp,
                                             bias=alibi_of(u, h, k - QT * s)).then_inc(e_done, 1)
                    if what == "OE":
                        act.wait_ge(pv_done, START + b * STEPS_B + steps_before(s, u) + ktiles(s))
                        act.wait_ge(at_done, START + g)
                        nc.scalar.activation(o_sb[:], ps_o[:], ACT.Copy).then_inc(o_copied, 1)
                        nc.scalar.activation(s_sb[:], ps_sum[:], ACT.Copy).then_inc(o_copied, 1)

            def alibi_of(u, h, dist_tiles):
                return alibi_c[:, bass.ds((u * GH + h) * (DIST0 + QT) + DIST0 + dist_tiles, 1)]

            alibi_c = alibi[:].rearrange("p h j -> p (h j)")
            act.wait_ge(vec_c, VEC_C)
            split_wq(0)
            walk(act, prologue, step, lambda b: None)

        @block.vector
        def _(dve):
            for h in range(NH):
                nc.vector.memset(slope[:, h:h + 1], slopes[h]).then_inc(vec_c, 1)
            nc.vector.memset(kexp[3 * DH:KR].bitcast(F32), 1.0).then_inc(vec_c, 1)
            dve.wait_ge(pool_c, 7)
            nc.vector.tensor_copy(dist[:], dist_i[:]).then_inc(vec_c, 1)
            nc.vector.tensor_copy(kmax[3 * DH:KR], kpos_i[3 * DH:KR]).then_inc(vec_c, 1)
            dve.wait_ge(vec_c, NH + 3)
            slope4_c = slope4[:].rearrange("p h t -> p (h t)")
            for t in range(QT):
                nc.vector.tensor_copy(slope4[:, :, t], slope[:]).then_inc(vec_c, 1)
            for h in range(NH):
                nc.vector.tensor_scalar(alibi[:, h], dist[:], slopes[h], None, ALU.mult).then_inc(vec_c, 1)
            dve.wait_ge(pe_c, 1)
            for t in range(QT):
                nc.vector.tensor_copy(slope_row[:, t * P:(t + 1) * P], ps_m[0:NH, 0:P]).then_inc(vec_c, 1)
            dve.wait_ge(wkv_in, 16)
            for r in range(3):
                nc.vector.tensor_copy(wkvh[:, :, r * DH:(r + 1) * DH], wkv_raw[:, :, 0:DH]).then_inc(vec_c, 1)
            nc.vector.tensor_copy(wkvh[:, :, 3 * DH:P], wkv_raw[:, :, DH:2 * DH]).then_inc(vec_c, 1)
            dve.wait_ge(vec_c, 2 * NH + 3 + 2 * QT + 4)
            for r in range(3):
                cols = slice(r * DH, (r + 1) * DH)
                nc.vector.tensor_tensor(wkvl[:, :, cols], wkv_raw[:, :, 0:DH], wkvh[:, :, cols].bitcast(F32),
                                        ALU.subtract).then_inc(vec_c, 1)
            nc.vector.tensor_tensor(wkvl[:, :, 3 * DH:P], wkv_raw[:, :, DH:2 * DH],
                                    wkvh[:, :, 3 * DH:P].bitcast(F32), ALU.subtract).then_inc(vec_c, 1)

            def split_x(b, s, j):
                n = DC * (b * NSEG + s) + j
                dve.wait_ge(xh_done, START + n + 1)
                nc.vector.tensor_tensor(xl[:, j], ps_m[:], xh[:, j].bitcast(F32), ALU.subtract).then_inc(xl_done, 1)

            def take_kv(b, s):
                sg = b * NSEG + s
                cols = slice(s * QB, (s + 1) * QB)
                dve.wait_ge(kv_ps, START + sg + 1)
                if s == 0:
                    dve.wait_ge(pv_done, START + b * STEPS_B)
                nc.vector.tensor_copy(kexp[0:3 * DH, cols], ps_m[0:3 * DH]).then_inc(kv_hi, 1)
                nc.vector.tensor_copy(vt_sb[3 * DH:P], ps_m[3 * DH:P]).then_inc(kv_hi, 1)
                dve.wait_ge(kv_hi, START + 2 * (sg + 1))
                nc.vector.tensor_tensor(kexp[DH:2 * DH, cols], ps_m[DH:2 * DH], kexp[DH:2 * DH, cols].bitcast(F32),
                                        ALU.subtract).then_inc(kv_lo, 1)
                dve.wait_ge(kv_lo, START + sg + 1)
                nc.vector.tensor_copy(kmax[0:3 * DH, cols], kexp[0:3 * DH, cols].bitcast(F32)).then_inc(kv_done, 1)

            def take_v(b, s):
                sg = b * NSEG + s
                dve.wait_ge(vt_ps, START + sg + 1)
                nc.vector.tensor_copy(val[:, s * QT:(s + 1) * QT], ps_m[:, 0:QT * DH].rearrange(
                    "p (t d) -> p t d", t=QT)).then_inc(vt_done, 1)

            def take_q(b, s, u, buf):
                g = unit_no(b, s, u)
                for h in range(GH):
                    dve.wait_ge(qh_done, START + GH * g + h + 1)
                    nc.vector.scalar_tensor_tensor(qst[buf][2 * DH:3 * DH, h], ps_m[h * DH:(h + 1) * DH], SCALE,
                                                   qst[buf][0:DH, h].bitcast(F32), ALU.mult,
                                                   ALU.subtract).then_inc(ql_done, 1)

            def maximum(b, s, u, i, chunk):
                h, t, c, cols = chunk
                dve.wait_ge(a_full, START + b * TILES_B + tiles_before(s, u) + i + 1)
                nc.vector.tensor_reduce(mxp[:, h * QT + t, c:c + 1], ps_a[i % 2][:, 0:cols], AX.X,
                                        ALU.max).then_inc(a_done, 1)

            def shifts(b, s, u):
                g = unit_no(b, s, u)
                dve.wait_ge(a_done, START + b * TILES_B + tiles_before(s, u) + GH * ktiles(s))
                nc.vector.tensor_reduce(mx[:], mxp[:, :, 0:s + 1], AX.X, ALU.max).then_inc(c_max, 1)
                dve.wait_ge(c_max, START + g + 1)
                nc.vector.scalar_tensor_tensor(shift[:], slope4_c[:, bass.ds(u * (GH * QT), GH * QT)], float(QB * s),
                                               mx[:], ALU.mult, ALU.subtract).then_inc(c_vec, 1)
                dve.wait_ge(c_ps, START + g + 1)
                dve.wait_ge(c_in, START + 16 * g)
                nc.vector.tensor_copy(shift_t[:], ps_m[0:GH * QT, 0:P]).then_inc(c_out, 1)

            def divide(g, part):
                if part < QT:
                    cols = slice(part * P, (part + 1) * P)
                    dve.wait_ge(o_copied, START + 2 * g)
                    nc.vector.reciprocal(r_sb[:, cols], s_sb[:, cols]).then_inc(r_done, 1)
                else:
                    dve.wait_ge(r_done, START + QT * g)
                    dve.wait_ge(at_out, START + 16 * (g - 1))
                    nc.vector.tensor_tensor(at_sb[:], o_sb[:], r_sb[:], ALU.mult).then_inc(at_done, 1)

            def prologue(b):
                for j in range(DC):
                    split_x(b, 0, j)
                take_kv(b, 0)
                take_v(b, 0)
                for u in range(2):
                    take_q(b, 0, u, u)
                for i, chunk in enumerate(a_chunks(0)):
                    maximum(b, 0, 0, i, chunk)
                shifts(b, 0, 0)

            def step(b, s, u, const, plan):
                i = 0
                for what, arg in plan:
                    if what == "X":
                        split_x(b, s + 1, arg)
                    if what == "KV":
                        take_kv(b, s + 1)
                    if what == "VT":
                        take_v(b, s + 1)
                    if what == "QE":
                        take_q(b, *ahead(s, u, 2, const), parity(s, const + 2))
                    if what == "A":
                        maximum(b, *ahead(s, u, 1, const), i, arg)
                        i += 1
                    if what == "C":
                        shifts(b, *ahead(s, u, 1, const))
                    if what == "R":
                        divide(unit_no(b, s, u), arg)

            def epilogue(b):
                for part in range(QT + 1):
                    divide(b * UB + UB, part)

            walk(dve, prologue, step, epilogue)

        @block.tensor
        def _(pe):
            pe.wait_ge(pool_c, 11)
            pe.wait_ge(vec_c, NH)
            nc.tensor.transpose(ps_m[0:NH, 0:P], slope[:], ident[:]).then_inc(pe_c, 1)
            pe.wait_ge(vec_c, VEC_C)

            def turn_x(b, s, j, g):
                sg = b * NSEG + s
                if j == 0:
                    pe.wait_ge(x_in, START + 16 * (sg + 1))
                    pe.wait_ge(c_out, START + g)
                else:
                    pe.wait_ge(xl_done, START + DC * sg + j)
                for t in range(QT):
                    last = nc.tensor.transpose(ps_m[:, t * P:(t + 1) * P], xs[:, t, j * P:(j + 1) * P], ident[:])
                last.then_inc(xt_ps, 1)

            def three(ps, wh, wl, mh, ml, start, stop):
                nc.tensor.matmul(ps, wh, mh, start=start, stop=False)
                nc.tensor.matmul(ps, wh, ml, start=False, stop=False)
                return nc.tensor.matmul(ps, wl, mh, start=False, stop=stop)

            def project_kv(b, s):
                sg = b * NSEG + s
                pe.wait_ge(xh_done, START + DC * (sg + 1))
                pe.wait_ge(xl_done, START + DC * (sg + 1))
                for j in range(DC):
                    last = three(ps_m[:], wkvh[:, j], wkvl[:, j], xh[:, j], xl[:, j], j == 0, j == DC - 1)
                last.then_inc(kv_ps, 1)

            def turn_v(b, s):
                sg = b * NSEG + s
                pe.wait_ge(kv_done, START + sg + 1)
                pe.sem_inc(went_on, 1)
                for t in range(QT):
                    last = nc.tensor.transpose(ps_m[:, t * DH:(t + 1) * DH], vt_sb[3 * DH:P, t * P:(t + 1) * P],
                                               ident[3 * DH:P, 3 * DH:P])
                last.then_inc(vt_ps, 1)

            def project_q(b, s, u, j):
                g = unit_no(b, s, u)
                if j == 0:
                    pe.wait_ge(wqh_done, START + g + 1)
                    pe.wait_ge(wql_done, START + g + 1)
                last = three(ps_m[:], wqh[:, j], wql[:, j], xh[:, j], xl[:, j], j == 0, j == DC - 1)
                if j == DC - 1:
                    last.then_inc(q_ps, 1)

            def scores_for_max(b, s, u, i, chunk, buf):
                h, t, c, cols = chunk
                ps = ps_a[i % 2]
                if i == 0:
                    g = unit_no(b, s, u)
                    pe.wait_ge(slope_in, START + 16 * (g + 1))
                    pe.wait_ge(again_in, START + 16 * (g + 1))
                    pe.wait_ge(ql_done, START + GH * (g + 1))
                    pe.wait_ge(kv_done, START + b * NSEG + s + 1)
                early = isinstance(u, int) and s == 0 and u == 0 and i < 2
                pe.wait_ge(a_done, START + b * TILES_B + (0 if early else tiles_before(s, u) + i - 1))
                last = nc.tensor.matmul(ps[:, 0:cols], qst[buf][0:KR, h, t * P:(t + 1) * P],
                                        kmax[0:KR, c * QB:c * QB + cols], start=True, stop=c < s)
                if c == s:
                    last = nc.tensor.matmul(ps[:, cols - P:cols], identb[:], maskb[:], start=False, stop=True)
                last.then_inc(a_full, 1)

            def turn_shift(b, s, u):
                pe.wait_ge(c_vec, START + unit_no(b, s, u) + 1)
                nc.tensor.transpose(ps_m[0:GH * QT, 0:P], shift[:], ident[:]).then_inc(c_ps, 1)

            def prologue(b):
                for j in range(DC):
                    turn_x(b, 0, j, b * UB)
                project_kv(b, 0)
                turn_v(b, 0)
                for u in range(2):
                    if u == 0:
                        pe.wait_ge(vt_done, START + b * NSEG + 1)
                    else:
                        pe.wait_ge(ql_done, START + GH * (b * UB + 1))
                    for j in range(DC):
                        project_q(b, 0, u, j)
                for i, chunk in enumerate(a_chunks(0)):
                    scores_for_max(b, 0, 0, i, chunk, 0)
                pe.wait_ge(ql_done, START + GH * (b * UB + 2))
                turn_shift(b, 0, 0)

            def step(b, s, u, const, plan):
                g = unit_no(b, s, u)
                buf = parity(s, const)
                i = 0
                for what, arg in plan:
                    if what == "X":
                        turn_x(b, s + 1, arg, g + 1)
                    if what == "KV":
                        project_kv(b, s + 1)
                    if what == "VT":
                        turn_v(b, s + 1)
                    if what == "Q":
                        if arg == 0 and ("VT", 0) in plan:
                            pe.wait_ge(vt_done, START + b * NSEG + s + 2)
                        elif arg == 0:
                            pe.wait_ge(c_out, START + g + 1)
                        project_q(b, *ahead(s, u, 2, const), arg)
                    if what == "A":
                        scores_for_max(b, *ahead(s, u, 1, const), i, arg, parity(s, const + 1))
                        i += 1
                    if what == "C":
                        if ("QE", 0) in plan:
                            pe.wait_ge(ql_done, START + GH * (g + 3))
                        else:
                            pe.wait_ge(c_out, START + g + 1)
                        turn_shift(b, *ahead(s, u, 1, const))
                    if what == "S":
                        k, h = arg
                        c0 = max(0, k - QT * s) * P
                        bank = parity_of(tiles_before(s, const) + GH * k + h)
                        if arg == (0, 0):
                            pe.wait_ge(c_in, START + 16 * (g + 1))
                        early = s == 0 and const == 0 and GH * k + h < 3
                        pe.wait_ge(e_done, START + b * TILES_B + (0 if early else tiles_before(s, u) + GH * k + h - 2))
                        diagonal = k >= QT * s
                        last = nc.tensor.matmul(ps_s[bank][:, c0:], kexp[0:KR, k * P:(k + 1) * P],
                                                qst[buf][0:KR, h, c0:], start=True, stop=not diagonal)
                        if diagonal:
                            last = nc.tensor.matmul(ps_s[bank][:, c0:c0 + P], identb[:], maskt[:], start=False,
                                                    stop=True)
                        last.then_inc(s_full, 1)
                    if what in ("PV", "SM"):
                        k = arg
                        c0 = max(0, k - QT * s) * P
                        slot = parity_of(steps_before(s, const) + k)
                        pe.wait_ge(e_done, START + b * TILES_B + tiles_before(s, u) + GH * (k + 1))
                        if k == 0 and what == "PV":
                            pe.wait_ge(vt_done, START + b * NSEG + s + 1)
                            pe.wait_ge(o_copied, START + 2 * g)
                        ps, weights = (ps_o, val[:, k]) if what == "PV" else (ps_sum, ones[:])
                        for h in range(GH):
                            last = nc.tensor.matmul(ps[h * DH:(h + 1) * DH, c0:], weights, prob[slot][:, h, c0:],
                                                    start=k == 0, stop=k == ktiles(s) - 1)
                        if what == "SM":
                            last.then_inc(pv_done, 1)

            walk(pe, prologue, step, lambda b: None)



def feed_forward(nc, sb, pb, sem, xt, ot, wo_v, w_v, bias, la, lb, gate_w, gate_b, att, ident):
    with ExitStack() as ctx:
        woh = sb(ctx, "woh", [P, DC, D], F32R)
        wol = sb(ctx, "wol", [P, DC, D], F32R)
        wth = sb(ctx, "wth", [P, DC, WX], F32R)
        wtl = sb(ctx, "wtl", [P, DC, WX], F32R)
        bth = sb(ctx, "bth", [RM, D], F32R)
        btl = sb(ctx, "btl", [RM, D], F32R)
        bias_b = sb(ctx, "bias_b", [P, D], F32)
        gate_bb = sb(ctx, "gate_bb", [P, NRK], F32)
        col_i = sb(ctx, "col_i", [P, RM], I32)
        col = sb(ctx, "col", [P, RM], F32)
        rank_step = sb(ctx, "rank_step", [P, NRK - 1], F32)
        at_raw = sb(ctx, "at_raw", [P, HG, P], F32)
        ath = [sb(ctx, f"ath{i}", [P, HG, P], F32R) for i in range(2)]
        atl = [sb(ctx, f"atl{i}", [P, HG, P], F32R) for i in range(2)]
        x_sb = sb(ctx, "x_sb", [P, D], F32)
        y_sb = sb(ctx, "y_sb", [P, D], F32)
        h_sb = sb(ctx, "h_sb", [P, D], F32)
        hb_sb = sb(ctx, "hb_sb", [P, D], F32)
        hth = sb(ctx, "hth", [P, DC, P], F32R)
        htl = sb(ctx, "htl", [P, DC, P], F32R)
        z_sb = [sb(ctx, f"z_sb{i}", [P, D], F32) for i in range(2)]
        stat = [sb(ctx, f"stat{i}", [P, 2, 6], F32) for i in range(2)]
        mv = [sb(ctx, f"mv{i}", [P, 2], F32) for i in range(2)]
        var = [sb(ctx, f"var{i}", [P, 1], F32) for i in range(2)]
        root = [sb(ctx, f"root{i}", [P, 1], F32) for i in range(2)]
        inv = [sb(ctx, f"inv{i}", [P, 1], F32) for i in range(2)]
        sq = [sb(ctx, f"sq{i}", [P, 1], F32) for i in range(2)]
        half = [sb(ctx, f"half{i}", [P, 1], F32) for i in range(2)]
        rstd = [sb(ctx, f"rstd{i}", [P, 1], F32) for i in range(2)]
        gate = sb(ctx, "gate", [P, NRK], F32)
        taken = sb(ctx, "taken", [P, NRK - 1], F32)
        width = sb(ctx, "width", [P, 1], F32)
        t_sb = sb(ctx, "t_sb", [P, RM], F32)
        tth = sb(ctx, "tth", [RM, P], F32R)
        ttl = sb(ctx, "ttl", [RM, P], F32R)

        ps_y = pb(ctx, "ps_y", [P, 2, 512])
        ps_t = pb(ctx, "ps_t", [P, 2, 512])
        ps_z = pb(ctx, "ps_z", [P, 3, 512])
        ps_l = pb(ctx, "ps_l", [P, 512])

        counters = []

        def counter(name):
            counters.append(sem(name))
            return counters[-1]

        went_on = sem("went_on_2")
        const_in = sem("const_in")
        f_c = sem("f_c")
        raw_in = [sem(f"raw_in{i}") for i in range(2)]
        raw_hi = sem("raw_hi")
        raw_lo = sem("raw_lo")
        raw_ps = sem("raw_ps")
        at_in = counter("at_in")
        ath_done = counter("ath_done")
        atl_done = counter("atl_done")
        x2_in = counter("x2_in")
        y_ps = counter("y_ps")
        y_done = counter("y_done")
        ln = [{n: counter(f"ln{i}_{n}") for n in ("stat", "mean", "var", "root", "inv", "sq", "half", "rstd")}
              for i in range(2)]
        h_done = counter("h_done")
        hb_done = counter("hb_done")
        t_ps = counter("t_ps")
        hth_done = counter("hth_done")
        htl_done = counter("htl_done")
        g_ps = counter("g_ps")
        g_vec = counter("g_vec")
        t_done = counter("t_done")
        l_ps = counter("l_ps")
        tth_done = counter("tth_done")
        ttl_done = counter("ttl_done")
        z_ps = counter("z_ps")
        z_done = counter("z_done")
        o_done = counter("o_done")
        o_out = [counter(f"o_out{i}") for i in range(2)]

        NZ = 3
        RAW = 2 * DC + 2

        def walk(eng, prologue, step):
            prologue()
            with eng.Fori(0, NTT // QT - 1) as a:
                for j in range(QT):
                    step(a * QT + j, a, j, True, True)
            for j in range(QT):
                step(NTT - QT + j, NTT // QT - 1, j, j + 1 < QT, j + 2 < QT)

        def if_used_wait(eng, n, par):
            if not (isinstance(n, int) and n < 2):
                eng.wait_ge(y_ps, START + n - 1)

        def tile_after(a, j, d):
            return a + (j + d) // QT, (j + d) % QT

        def turned(ps):
            return ps[:].rearrange("p a (k r) -> p (a k) r", r=P)

        def piece(p):
            return slice(p * WCH, (p + 1) * WCH)

        last_piece = D - (NZ - 1) * WCH
        with nc.Block() as start:
            @start.sync
            def _(sp):
                for c in counters:
                    sp.sem_inc(c, START)

        block = ctx.enter_context(nc.Block())

        @block.sync
        def _(sp):
            sp.dma_start(bias_b[:], bias.partition_broadcast(P)).then_inc(const_in, 16)
            sp.dma_start(gate_bb[:], gate_b.partition_broadcast(P)).then_inc(const_in, 16)
            for c in range(RAW):
                if c >= 2:
                    sp.wait_ge(raw_lo, c - 1)
                raw = z_sb[c % 2]
                if c < DC:
                    sp.dma_start(raw[:], wo_v[c]).then_inc(raw_in[c % 2], 16)
                elif c < 2 * DC:
                    sp.dma_start(raw[:], w_v[c - DC]).then_inc(raw_in[c % 2], 16)
                elif c == 2 * DC:
                    sp.dma_start(raw[0:RM], la).then_inc(raw_in[c % 2], 16)
                    sp.dma_start(raw[RM:RM + NRK], gate_w).then_inc(raw_in[c % 2], 16)
                else:
                    sp.dma_start(raw[:, 0:DC * RM].rearrange("p (o r) -> p o r", o=DC),
                                 lb.rearrange("(o p) r -> p o r", p=P)).then_inc(raw_in[c % 2], 16)

            def load_at(n, a, t):
                sp.wait_ge(ath_done, START + n)
                sp.wait_ge(atl_done, START + n)
                sp.dma_start(at_raw[:], att_tiles[a, t]).then_inc(at_in, 16)

            def load_x(n):
                sp.wait_ge(y_done, START + n)
                sp.dma_start(x_sb[:], xt[n]).then_inc(x2_in, 16)

            att_tiles = att.rearrange("(a g) t p q -> a t p g q", g=HG)

            def prologue():
                load_at(0, 0, 0)
                load_x(0)
                load_at(1, 0, 1)

            def step(n, a, j, has_next, has_after):
                if has_next:
                    load_x(n + 1)
                if has_after:
                    load_at(n + 2, *tile_after(a, j, 2))
                sp.wait_ge(o_done, START + n + 1)
                sp.dma_start(ot[n], z_sb[j % 2][:]).then_inc(o_out[j % 2], 16)

            walk(sp, prologue, step)
            for par in range(2):
                sp.wait_ge(o_out[par], START + 16 * NTT // 2)

        @block.gpsimd
        def _(pool):
            nc.gpsimd.iota(col_i[:], [[1, RM]], base=-RANKS[0], channel_multiplier=0).then_inc(f_c, 1)
            for r in range(NRK - 1):
                nc.gpsimd.memset(rank_step[:, r:r + 1], float(RANKS[r + 1] - RANKS[r])).then_inc(f_c, 1)
            pool.wait_ge(const_in, 32)

            def add_bias(n):
                pool.wait_ge(h_done, START + n + 1)
                pool.wait_ge(z_done, START + 2 * n)
                nc.gpsimd.tensor_tensor(hb_sb[:], h_sb[:], bias_b[:], ALU.add).then_inc(hb_done, 1)

            walk(pool, lambda: add_bias(0),
                 lambda n, a, j, has_next, has_after: add_bias(n + 1) if has_next else None)

        @block.scalar
        def _(act):
            for c in range(RAW):
                if c < DC:
                    act.wait_ge(raw_in[c % 2], 16 * (c // 2 + 1))
                    nc.scalar.activation(woh[:, c], z_sb[c % 2][:], ACT.Copy).then_inc(raw_hi, 1)
                else:
                    act.wait_ge(raw_ps, c - DC + 1)
                    src = turned(ps_t if c % 2 else ps_y)
                    if c < 2 * DC:
                        o = c - DC
                        nc.scalar.activation(wth[:, :, o * P:(o + 1) * P], src, ACT.Copy).then_inc(raw_hi, 1)
                    elif c == 2 * DC:
                        nc.scalar.activation(wth[:, :, D:WX], src[:, :, 0:RM + NRK], ACT.Copy).then_inc(raw_hi, 1)
                    else:
                        nc.scalar.activation(bth[:].rearrange("r (o p) -> r o p", p=P), src[0:RM],
                                             ACT.Copy).then_inc(raw_hi, 1)

            def split_at(n, par):
                act.wait_ge(at_in, START + 16 * (n + 1))
                if_used_wait(act, n, par)
                nc.scalar.activation(ath[par][:], at_raw[:], ACT.Copy).then_inc(ath_done, 1)

            def take_root(i, n):
                act.wait_ge(ln[i]["var"], START + n + 1)
                nc.scalar.activation(root[i][:], var[i][:], ACT.Sqrt).then_inc(ln[i]["root"], 1)

            def prologue():
                split_at(0, 0)
                split_at(1, 1)
                take_root(0, 0)

            def step(n, a, j, has_next, has_after):
                act.wait_ge(t_ps, START + n + 1)
                nc.scalar.activation(hth[:], turned(ps_t), ACT.Copy).then_inc(hth_done, 1)
                if has_next:
                    take_root(0, n + 1)
                act.wait_ge(l_ps, START + n + 1)
                nc.scalar.activation(tth[:], ps_l[0:RM, 0:P], ACT.Copy).then_inc(tth_done, 1)
                if has_after:
                    split_at(n + 2, j % 2)
                take_root(1, n)

            walk(act, prologue, step)

        @block.vector
        def _(dve):
            for c in range(RAW):
                dve.wait_ge(raw_hi, c + 1)
                src = turned(ps_t if c % 2 else ps_y)
                if c < DC:
                    nc.vector.tensor_tensor(wol[:, c], z_sb[c % 2][:], woh[:, c].bitcast(F32),
                                            ALU.subtract).then_inc(raw_lo, 1)
                elif c < 2 * DC:
                    cols = slice((c - DC) * P, (c - DC + 1) * P)
                    nc.vector.tensor_tensor(wtl[:, :, cols], src, wth[:, :, cols].bitcast(F32),
                                            ALU.subtract).then_inc(raw_lo, 1)
                elif c == 2 * DC:
                    nc.vector.tensor_tensor(wtl[:, :, D:WX], src[:, :, 0:RM + NRK], wth[:, :, D:WX].bitcast(F32),
                                            ALU.subtract).then_inc(raw_lo, 1)
                else:
                    nc.vector.tensor_tensor(btl[:].rearrange("r (o p) -> r o p", p=P), src[0:RM],
                                            bth[:].rearrange("r (o p) -> r o p", p=P).bitcast(F32),
                                            ALU.subtract).then_inc(raw_lo, 1)
            dve.wait_ge(f_c, NRK)
            nc.vector.tensor_copy(col[:], col_i[:]).then_inc(f_c, 1)
            dve.wait_ge(f_c, NRK + 1)
            dve.wait_ge(const_in, 32)

            def split_at(n, par):
                dve.wait_ge(ath_done, START + n + 1)
                if_used_wait(dve, n, par)
                nc.vector.tensor_tensor(atl[par][:], at_raw[:], ath[par][:].bitcast(F32),
                                        ALU.subtract).then_inc(atl_done, 1)

            def norm(i, n, src, dst, done):
                s = ln[i]
                for k in range(2):
                    nc.vector.bn_stats(stat[i][:, k], src[:, k * 512:(k + 1) * 512]).then_inc(s["stat"], 1)
                dve.wait_ge(s["stat"], START + 2 * (n + 1))
                dve.sem_inc(went_on, 1)
                nc.vector.bn_aggr(mv[i][:], stat[i][:].rearrange("p a k -> p (a k)")).then_inc(s["mean"], 1)
                dve.wait_ge(s["mean"], START + n + 1)
                nc.vector.tensor_scalar(var[i][:], mv[i][:, 1:2], EPS, None, ALU.add).then_inc(s["var"], 1)
                dve.wait_ge(s["root"], START + n + 1)
                nc.vector.reciprocal(inv[i][:], root[i][:]).then_inc(s["inv"], 1)
                dve.wait_ge(s["inv"], START + n + 1)
                nc.vector.tensor_tensor(sq[i][:], inv[i][:], inv[i][:], ALU.mult).then_inc(s["sq"], 1)
                dve.wait_ge(s["sq"], START + n + 1)
                nc.vector.scalar_tensor_tensor(half[i][:], sq[i][:], -0.5, var[i][:], ALU.mult,
                                               ALU.mult).then_inc(s["half"], 1)
                dve.wait_ge(s["half"], START + n + 1)
                nc.vector.scalar_tensor_tensor(rstd[i][:], half[i][:], 1.5, inv[i][:], ALU.add,
                                               ALU.mult).then_inc(s["rstd"], 1)
                dve.wait_ge(s["rstd"], START + n + 1)
                nc.vector.tensor_scalar(dst, src, mv[i][:, 0:1], rstd[i][:, 0:1], ALU.subtract,
                                        ALU.mult).then_inc(done, 1)

            def first_norm(n):
                dve.wait_ge(y_ps, START + n + 1)
                dve.wait_ge(x2_in, START + 16 * (n + 1))
                nc.vector.tensor_tensor(y_sb[:], ps_y[:].rearrange("p a n -> p (a n)"), x_sb[:],
                                        ALU.add).then_inc(y_done, 1)
                dve.wait_ge(y_done, START + n + 1)
                dve.wait_ge(t_ps, START + n)
                dve.wait_ge(hb_done, START + n)
                norm(0, n, y_sb[:], h_sb[:], h_done)

            def choose(n):
                dve.wait_ge(g_ps, START + n + 1)
                g = ps_z[:, NZ - 1, last_piece + RM:WCH]
                nc.vector.tensor_tensor(gate[:], g, gate_bb[:], ALU.add).then_inc(g_vec, 1)
                for r in range(1, NRK):
                    dve.wait_ge(g_vec, START + (NRK + 1) * n + r)
                    nc.vector.tensor_tensor(gate[:, r:r + 1], gate[:, r - 1:r], gate[:, r:r + 1],
                                            ALU.max).then_inc(g_vec, 1)
                dve.wait_ge(g_vec, START + (NRK + 1) * n + NRK)
                nc.vector.scalar_tensor_tensor(taken[:], gate[:, 0:NRK - 1], gate[:, NRK - 1:NRK], rank_step[:],
                                               ALU.is_lt, ALU.mult, accum_out=width[:]).then_inc(g_vec, 1)
                dve.wait_ge(g_vec, START + (NRK + 1) * (n + 1))
                nc.vector.scalar_tensor_tensor(t_sb[:], col[:], width[:, 0:1],
                                               ps_z[:, NZ - 1, last_piece:last_piece + RM],
                                               ALU.is_lt, ALU.mult).then_inc(t_done, 1)
                dve.wait_ge(tth_done, START + n + 1)
                nc.vector.tensor_tensor(ttl[:], ps_l[0:RM, 0:P], tth[:].bitcast(F32),
                                        ALU.subtract).then_inc(ttl_done, 1)

            def second_norm(n, j, stored):
                z = z_sb[j % 2]
                dve.wait_ge(z_ps, START + n + 1)
                dve.wait_ge(hb_done, START + n + 1)
                dve.wait_ge(o_out[j % 2], START + 16 * stored)
                cut = (NZ - 1) * WCH
                nc.vector.tensor_tensor(z[:, 0:cut].rearrange("p (a n) -> p a n", n=WCH), ps_z[:, 0:NZ - 1, 0:WCH],
                                        hb_sb[:, 0:cut].rearrange("p (a n) -> p a n", n=WCH),
                                        ALU.add).then_inc(z_done, 1)
                nc.vector.tensor_tensor(z[:, cut:D], ps_z[:, NZ - 1, 0:last_piece], hb_sb[:, cut:D],
                                        ALU.add).then_inc(z_done, 1)
                dve.wait_ge(z_done, START + 2 * (n + 1))
                norm(1, n, z[:], z[:], o_done)

            def prologue():
                split_at(0, 0)
                split_at(1, 1)
                first_norm(0)

            def step(n, a, j, has_next, has_after):
                dve.wait_ge(hth_done, START + n + 1)
                nc.vector.tensor_tensor(htl[:], turned(ps_t), hth[:].bitcast(F32), ALU.subtract).then_inc(htl_done, 1)
                if has_next:
                    first_norm(n + 1)
                choose(n)
                if has_after:
                    split_at(n + 2, j % 2)
                second_norm(n, j, a * (QT // 2) + j // 2)

            walk(dve, prologue, step)

        @block.tensor
        def _(pe):
            for c in range(DC, RAW):
                pe.wait_ge(raw_in[c % 2], 16 * (c // 2 + (2 if c == 2 * DC else 1)))
                pe.wait_ge(raw_lo, c - 1)
                raw, ps = z_sb[c % 2], ps_t if c % 2 else ps_y
                for k in range(DC):
                    dst = ps[:, k // QT, (k % QT) * P:(k % QT + 1) * P]
                    if c < 2 * DC:
                        last = nc.tensor.transpose(dst, raw[:, k * P:(k + 1) * P], ident[:])
                    elif c == 2 * DC:
                        last = nc.tensor.transpose(dst[:, 0:RM + NRK], raw[0:RM + NRK, k * P:(k + 1) * P],
                                                   ident[0:RM + NRK, 0:RM + NRK])
                    else:
                        last = nc.tensor.transpose(dst[0:RM], raw[:, k * RM:(k + 1) * RM], ident[:])
                last.then_inc(raw_ps, 1)
            pe.wait_ge(raw_lo, RAW)

            def first_product(n, par):
                pe.wait_ge(ath_done, START + n + 1)
                pe.wait_ge(atl_done, START + n + 1)
                pe.wait_ge(y_done, START + n)
                for half_no in range(2):
                    cols = slice(half_no * 512, (half_no + 1) * 512)
                    ps = ps_y[:, half_no]
                    for c in range(HG):
                        first, end = c == 0, c == HG - 1
                        nc.tensor.matmul(ps, ath[par][:, c], woh[:, c, cols], start=first, stop=False)
                        nc.tensor.matmul(ps, ath[par][:, c], wol[:, c, cols], start=False, stop=False)
                        last = nc.tensor.matmul(ps, atl[par][:, c], woh[:, c, cols], start=False, stop=end)
                last.then_inc(y_ps, 1)

            def second_product(n, p):
                ps = ps_z[:, p, 0:WCH]
                for c in range(DC):
                    nc.tensor.matmul(ps, hth[:, c], wth[:, c, piece(p)], start=c == 0, stop=False,
                                     skip_group_check=True)
                    nc.tensor.matmul(ps, hth[:, c], wtl[:, c, piece(p)], start=False, stop=False,
                                     skip_group_check=True)
                    last = nc.tensor.matmul(ps, htl[:, c], wth[:, c, piece(p)], start=False, stop=False,
                                            skip_group_check=True)
                return last

            def step(n, a, j, has_next, has_after):
                pe.wait_ge(h_done, START + n + 1)
                pe.wait_ge(htl_done, START + n)
                for k in range(DC):
                    last = nc.tensor.transpose(ps_t[:, k // QT, (k % QT) * P:(k % QT + 1) * P],
                                               h_sb[:, k * P:(k + 1) * P], ident[:])
                last.then_inc(t_ps, 1)
                if has_next:
                    first_product(n + 1, (j + 1) % 2)
                pe.wait_ge(hth_done, START + n + 1)
                pe.wait_ge(htl_done, START + n + 1)
                pe.wait_ge(z_done, START + 2 * n)
                second_product(n, NZ - 1).then_inc(g_ps, 1)
                second_product(n, 0)
                pe.wait_ge(t_done, START + n + 1)
                pe.wait_ge(ttl_done, START + n)
                pe.sem_inc(went_on, 1)
                nc.tensor.transpose(ps_l[0:RM, 0:P], t_sb[:], ident[:]).then_inc(l_ps, 1)
                second_product(n, 1)
                pe.wait_ge(tth_done, START + n + 1)
                pe.wait_ge(ttl_done, START + n + 1)
                for p in range(NZ):
                    cols = slice(p * WCH, min(D, (p + 1) * WCH))
                    ps = ps_z[:, p, 0:cols.stop - cols.start]
                    nc.tensor.matmul(ps, tth[:], bth[:, cols], start=False, stop=False, skip_group_check=True)
                    nc.tensor.matmul(ps, tth[:], btl[:, cols], start=False, stop=False, skip_group_check=True)
                    last = nc.tensor.matmul(ps, ttl[:], bth[:, cols], start=False, stop=True,
                                            skip_group_check=True)
                last.then_inc(z_ps, 1)

            walk(pe, lambda: first_product(0, 0), step)


_INS = ["L0_attn_hidden_states", "L0_attn_Wq", "L0_attn_Wkv", "L0_attn_Wo", "L0_ffn_W", "L0_ffn_b", "L0_ffn_A",
        "L0_ffn_B", "L0_ffn_gate_w", "L0_ffn_gate_b"]


def kernel(**inputs):
    import concourse.bacc as bacc
    from concourse.bass_utils import run_bass_kernel_spmd

    nc = bacc.Bacc("TRN2", target_bir_lowering=False, num_devices=1)
    arrays, args = {}, []
    for name in _INS:
        a = np.ascontiguousarray(inputs[name])
        arrays[f"in_{name}"] = a
        args.append(nc.dram_tensor(f"in_{name}", a.shape, mybir.dt.from_np(a.dtype), kind="ExternalInput").ap())
    out = nc.dram_tensor("out", (B, T, D), F32, kind="ExternalOutput").ap()
    program(nc, *args, out)
    r = run_bass_kernel_spmd(nc, [arrays], core_ids=[0])
    return r.results[0]["out"]
```

```python
from contextlib import ExitStack

import numpy as np
import concourse.bass as bass
from concourse import mybir

ALU = mybir.AluOpType
ACT = mybir.ActivationFunctionType
AX = mybir.AxisListType
F32 = mybir.dt.float32
F32R = mybir.dt.float32r
BF16 = mybir.dt.bfloat16
I32 = mybir.dt.int32

P = 128
B, T, D = 2, 2048, 1024
NH, DH = 32, 32
DC = D // P
GH = P // DH
HG = NH // GH
QB = 512
NSEG = T // QB
QT = QB // P
SCALE = DH ** -0.5
EPS = 1e-5
MASKED = -1.0e30
START = 1
PROBS = 6
KR = 3 * DH + 1
RANKS = (8, 16, 32, 64)
NRK = len(RANKS)
RM = max(RANKS)
WX = D + RM + NRK
WCH = WX // 3
NTT = B * T // P
DIST0 = NSEG * QT - QT



def alibi_slopes(n):
    start = 2.0 ** (-2.0 ** (-(np.log2(n) - 3)))
    return [float(np.float32(start ** (i + 1))) for i in range(n)]


def ktiles(s):
    return QT * (s + 1)


TILES_B = HG * GH * sum(ktiles(s) for s in range(NSEG))
STEPS_B = TILES_B // GH


def tiles_before(s, u):
    return HG * GH * sum(ktiles(x) for x in range(s)) + u * (GH * ktiles(s))


def steps_before(s, u):
    return HG * sum(ktiles(x) for x in range(s)) + u * ktiles(s)


def pairs_summed(s):
    return ktiles(s) // 2 - 1 if s else 0


PAIRS_B = HG * sum(pairs_summed(s) for s in range(NSEG))


def pairs_before(s, u):
    return HG * sum(pairs_summed(x) for x in range(s)) + u * pairs_summed(s)


def parity(s, u0, n=3):
    return (HG * s + u0) % n


def bank_of(count):
    return count % 3


def slot_of(count):
    return count % PROBS


def a_chunks(s):
    return [(h, t, c, QB if c < s else (t + 1) * P) for c in range(s + 1) for h in range(GH) for t in range(QT)]


Q_SPACE = 0.5
X_SPACE = (1, 1.5, 2.5, 2.5)
RECIP_AT = ((2, 4, 6, 8, 9), (5, 19, 28, 29, 30), (14, 26, 44, 45, 46), (20, 36, 60, 61, 62))


def plan_step(s, has_a, sa, has_q, prep, has_r):
    n = ktiles(s)
    slots = n * GH
    chunks = a_chunks(sa) if has_a else []
    a_slots = slots - (7 if s else 6)
    at = {}
    for i, x in enumerate(chunks):
        at.setdefault(i * a_slots // len(chunks), []).append(("A", x))
    if has_a:
        at.setdefault(a_slots, []).append(("CV", 0))
        at.setdefault(a_slots + 2, []).append(("CT", 0))
    space = X_SPACE[s]
    misc = [(space, ("X", j)) for j in range(DC)] + [(1, ("KV", 0)), (space, ("VT", 0))] if prep else []
    if has_q:
        misc += [(1 if s else Q_SPACE, ("Q", j)) for j in range(DC)]
        misc += [(min(s + 1, 3), ("QE", h)) for h in range(GH)]
    place = 1.0
    for width, x in misc:
        at.setdefault(min(a_slots - 1, int(place)), []).append(x)
        place += width
    if has_q:
        at.setdefault(min(a_slots - 1, int(place)) if s else slots - 1, []).append(("WS", 0))
    out = []
    recip_at = {x: part for part, x in enumerate(RECIP_AT[s])}
    summed = pairs_summed(s)
    for k in range(n):
        for h in range(GH):
            i = k * GH + h
            out += [x for x in at.get(i, []) if x[0] == "X"]
            out.append(("S", (k, h)))
            if has_r and i in recip_at:
                out.append(("R", recip_at[i]))
            out += [x for x in at.get(i, []) if x[0] != "X"]
            if k and h == 1:
                out.append(("PV", k - 1))
            if h == 3 and k > 2 * summed:
                out.append(("SM", k - 1))
            if h == 3 and k >= 4 and k % 2 == 0 and k // 2 - 2 < summed:
                out.append(("SP", k // 2 - 2))
        if k % 2 and k // 2 < summed:
            out.append(("ADD", k // 2))
    if summed:
        out.append(("SP", summed - 1))
    out += [("PV", n - 1), ("SM", n - 1)]
    out.append(("OE", 0))
    return out


def program(nc, x, wq, wkv, wo, w, bias, la, lb, gate_w, gate_b, out):
    nc.disable_value_cache = True
    slopes = alibi_slopes(NH)
    att = nc.dram_tensor("att_scratch", (B * NSEG * HG, QT, P, P), F32, kind="Internal").ap()
    slope_rows = nc.dram_tensor("slope_rows", (NH, QB), F32, kind="Internal").ap()

    xb = x.rearrange("b (s t p) d -> b s p t d", t=QT, p=P)
    xt = x.rearrange("b (i p) d -> (b i) p d", p=P)
    ot = out.rearrange("b (i p) d -> (b i) p d", p=P)
    wq_v = wq.rearrange("(c p) (g m) -> g p c m", p=P, m=P)
    wo_v = wo.rearrange("(c p) n -> c p n", p=P)
    w_v = w.rearrange("(o p) n -> o p n", p=P)

    with ExitStack() as ctx:
        def sem(name):
            return ctx.enter_context(nc.semaphore(name))

        def sb(c, name, shape, dt):
            return c.enter_context(nc.sbuf_tensor(name, shape, dt))

        def pb(c, name, shape, dt=F32):
            return c.enter_context(nc.psum_tensor(name, shape, dt))

        ident = sb(ctx, "ident", [P, P], F32)
        attention(nc, sb, pb, sem, slopes, xb, wq_v, wkv, att, slope_rows, ident)
        feed_forward(nc, sb, pb, sem, xt, ot, wo_v, w_v, bias, la, lb, gate_w, gate_b, att, ident)


def attention(nc, sb, pb, sem, slopes, xb, wq_v, wkv, att, slope_rows, ident):
    with ExitStack() as ctx:
        identb = sb(ctx, "identb", [P, P], BF16)
        maskb = sb(ctx, "maskb", [P, P], BF16)
        maskt = sb(ctx, "maskt", [P, P], BF16)
        ones = sb(ctx, "ones", [P, DH], F32)
        slope = sb(ctx, "slope", [P, NH], F32)
        slope4 = sb(ctx, "slope4", [P, NH, QT], F32)
        dist_i = sb(ctx, "dist_i", [P, DIST0 + QT], I32)
        dist = sb(ctx, "dist", [P, DIST0 + QT], F32)
        alibi = sb(ctx, "alibi", [P, NH, DIST0 + QT], F32)
        slope_row = sb(ctx, "slope_row", [NH, QB], F32R)
        kpos_i = sb(ctx, "kpos_i", [P, T], I32)
        xs = sb(ctx, "xs", [P, QT, D], F32)
        xh = sb(ctx, "xh", [P, DC, QB], F32R)
        xl = sb(ctx, "xl", [P, DC, QB], F32R)
        wkv_raw = sb(ctx, "wkv_raw", [P, DC, 2 * DH], F32)
        wkvh = sb(ctx, "wkvh", [P, DC, P], F32R)
        wkvl = sb(ctx, "wkvl", [P, DC, P], F32R)
        wq_raw = sb(ctx, "wq_raw", [P, DC, P], F32)
        wqh = sb(ctx, "wqh", [P, DC, P], F32R)
        wql = sb(ctx, "wql", [P, DC, P], F32R)
        kmax = sb(ctx, "kmax", [P, T], F32R)
        kexp = sb(ctx, "kexp", [P, T], F32R)
        vt_sb = sb(ctx, "vt_sb", [P, QB], F32)
        val = sb(ctx, "val", [P, T // P, DH], F32)
        qst = [sb(ctx, f"qst{i}", [P, GH, QB], F32R) for i in range(3)]
        mxp = sb(ctx, "mxp", [P, GH * QT, NSEG], F32)
        mx = sb(ctx, "mx", [P, GH * QT], F32)
        shift = sb(ctx, "shift", [P, GH * QT], F32)
        shift_t = sb(ctx, "shift_t", [GH * QT, P], F32R)
        prob = [sb(ctx, f"prob{i}", [P, GH, QB], F32) for i in range(PROBS)]
        o_sb = sb(ctx, "o_sb", [P, QB], F32)
        s_sb = sb(ctx, "s_sb", [P, QB], F32)
        r_sb = sb(ctx, "r_sb", [P, QB], F32)
        at_sb = sb(ctx, "at_sb", [P, QB], F32)

        ps_s = [pb(ctx, f"ps_s{i}", [P, QB]) for i in range(2)]
        ps_a = [pb(ctx, f"ps_a{i}", [P, QB]) for i in range(3)]
        ps_o = pb(ctx, "ps_o", [P, QB])
        ps_sum = pb(ctx, "ps_sum", [P, QB])
        ps_m = pb(ctx, "ps_m", [P, QB])

        def turned_in(s, j):
            return ps_m if s else ps_a[j % 2]

        counters = []

        def counter(name):
            counters.append(sem(name))
            return counters[-1]

        pool_c = sem("pool_c")
        vec_c = sem("vec_c")
        pe_c = sem("pe_c")
        rows_out = sem("rows_out")
        wkv_in = sem("wkv_in")
        went_on = sem("went_on")
        x_in = counter("x_in")
        wq_in = counter("wq_in")
        xt_ps = counter("xt_ps")
        xh_done = counter("xh_done")
        xl_done = counter("xl_done")
        kv_ps = counter("kv_ps")
        kv_hi = counter("kv_hi")
        kv_lo = counter("kv_lo")
        kv_done = counter("kv_done")
        vt_ps = counter("vt_ps")
        vt_done = counter("vt_done")
        wqh_done = counter("wqh_done")
        wql_done = counter("wql_done")
        q_ps = counter("q_ps")
        qh_done = counter("qh_done")
        ql_done = counter("ql_done")
        stack_in = counter("stack_in")
        c_max = counter("c_max")
        c_vec = counter("c_vec")
        c_ps = counter("c_ps")
        c_out = counter("c_out")
        c_in = counter("c_in")
        o_copied = counter("o_copied")
        r_done = counter("r_done")
        at_done = counter("at_done")
        at_out = counter("at_out")
        s_full = counter("s_full")
        e_done = counter("e_done")
        a_full = counter("a_full")
        a_done = counter("a_done")
        pv_done = counter("pv_done")
        pair_done = counter("pair_done")
        sm_done = counter("sm_done")
        VEC_C = 2 * NH + 3 + 2 * QT + 8
        UB = NSEG * HG

        def walk(eng, prologue, unit_step, epilogue):
            with eng.Fori(0, B) as b:
                prologue(b)
                for s in range(NSEG):
                    more = s + 1 < NSEG
                    if s == 0:
                        for u in range(HG - 2):
                            unit_step(b, s, u, u, plan_step(s, True, s, True, False, u > 0))
                    else:
                        with eng.Fori(0, 2) as i:
                            for j in range(3):
                                unit_step(b, s, i * 3 + j, j, plan_step(s, True, s, True, False, True))
                    unit_step(b, s, HG - 2, HG - 2, plan_step(s, True, s, more, more, True))
                    unit_step(b, s, HG - 1, HG - 1, plan_step(s, more, s + 1, more, False, True))
                epilogue(b)

        def ahead(s, u, d, const):
            return (s, u + d) if const + d < HG else (s + 1, const + d - HG)

        def unit_no(b, s, u):
            return b * UB + (HG * s) + u

        taken = []

        def counts(eng, b, s, u):
            taken.append(eng)
            values = (unit_no(b, s, u), START + b * TILES_B + tiles_before(s, u),
                      START + b * STEPS_B + steps_before(s, u))
            regs = [eng.alloc_register(f"{name}_{len(taken)}") for name in ("unit", "tiles", "steps")]
            for reg, value in zip(regs, values):
                eng.reg_mov(reg, value)
            return tuple(eng.snap(reg, min_val=low) for reg, low in zip(regs, (0, START, START)))

        with nc.Block() as start:
            @start.sync
            def _(sp):
                for c in counters:
                    sp.sem_inc(c, START)

        block = ctx.enter_context(nc.Block())

        @block.sync
        def _(sp):
            sp.dma_start(wkv_raw[:], wkv.rearrange("(c p) m -> p c m", p=P)).then_inc(wkv_in, 16)
            sp.wait_ge(vec_c, 2 * NH + 3 + 2 * QT)
            sp.dma_start(slope_rows, slope_row[:].bitcast(F32)).then_inc(rows_out, 16)
            sp.wait_ge(rows_out, 16)

            def last_row(buf):
                return qst[buf][3 * DH:KR].bitcast(F32)

            def load_x(b, s, batch=None):
                sp.wait_ge(xt_ps, START + DC * (b * NSEG + s))
                sp.dma_start(xs[:], xb[b, s] if batch is None else xb[batch, 0]).then_inc(x_in, 16)

            def load_wq(number, u):
                sp.wait_ge(wql_done, START + number)
                sp.dma_start(wq_raw[:], wq_v[u]).then_inc(wq_in, 16)

            def put_slopes(b, s, u, buf, old_tiles):
                g = unit_no(b, s, u)
                sp.wait_ge(s_full, START + old_tiles)
                sp.wait_ge(stack_in, START + 32 * g)
                rows = slope_rows[bass.ds(u * GH, GH)].rearrange("(a h) t -> a h t", a=1)
                sp.dma_start(last_row(buf), rows).then_inc(stack_in, 16)

            def repeat_q(b, s, u, buf):
                g = unit_no(b, s, u)
                sp.wait_ge(ql_done, START + GH * (g + 1))
                sp.dma_start(qst[buf][DH:2 * DH].bitcast(F32), qst[buf][0:DH].bitcast(F32)).then_inc(stack_in, 16)

            def put_shift(b, s, u, buf):
                sp.wait_ge(c_out, START + unit_no(b, s, u) + 1)
                sp.dma_start(last_row(buf), shift_t[:].bitcast(F32)).then_inc(c_in, 16)

            def store_before(g):
                sp.wait_ge(at_done, START + g)
                sp.dma_start(att[g - 1].rearrange("t p q -> p t q"),
                             at_sb[:].rearrange("p (t q) -> p t q", t=QT)).then_inc(at_out, 16)

            def prologue(b):
                for u in range(2):
                    put_slopes(b, 0, u, u, b * TILES_B)
                    load_wq(b * UB + u + 1, u + 1)
                    repeat_q(b, 0, u, u)
                put_shift(b, 0, 0, 0)

            def step(b, s, u, const, plan):
                if ("QE", 0) in plan:
                    s2, u2 = ahead(s, u, 2, const)
                    old = b * TILES_B + tiles_before(s, u)
                    put_slopes(b, s2, u2, parity(s, const + 2), old)
                    load_wq(unit_no(b, s, u) + 3, (u + 3) % HG)
                if s == 0 and const == 0:
                    load_x(b, 1)
                if const == HG - 1 and s + 2 < NSEG:
                    load_x(b, s + 2)
                for what, arg in plan:
                    if what == "R" and arg == QT:
                        store_before(unit_no(b, s, u))
                    if what == "QE" and arg == GH - 1:
                        repeat_q(b, s2, u2, parity(s, const + 2))
                    if what == "CT":
                        s1, u1 = ahead(s, u, 1, const)
                        put_shift(b, s1, u1, parity(s, const + 1))

            def epilogue(b):
                load_x(b, NSEG, (b + 1) % B)
                store_before(b * UB + UB)

            sp.dma_start(xs[:], xb[0, 0]).then_inc(x_in, 16)
            sp.dma_start(wq_raw[:], wq_v[0]).then_inc(wq_in, 16)
            walk(sp, prologue, step, epilogue)
            sp.wait_ge(wq_in, START + 16 * (B * UB + 1))
            sp.wait_ge(at_out, START + 16 * B * UB)
            sp.wait_ge(x_in, START + 16 * (B * NSEG + 1))

        @block.gpsimd
        def _(pool):
            nc.gpsimd.memset(ident[:], 0.0).then_inc(pool_c, 1)
            nc.gpsimd.memset(identb[:], 0.0).then_inc(pool_c, 1)
            nc.gpsimd.memset(maskb[:], 0.0).then_inc(pool_c, 1)
            nc.gpsimd.memset(maskt[:], 0.0).then_inc(pool_c, 1)
            nc.gpsimd.memset(ones[:], 1.0).then_inc(pool_c, 1)
            nc.gpsimd.iota(dist_i[:], [[P, DIST0 + QT]], base=-P * DIST0, channel_multiplier=1).then_inc(pool_c, 1)
            pool.wait_ge(pool_c, 6)
            nc.gpsimd.iota(kpos_i[3 * DH:KR], [[1, T]], base=0, channel_multiplier=0).then_inc(pool_c, 1)
            pool.wait_ge(pool_c, 7)
            for m in (ident, identb):
                nc.gpsimd.affine_select(out=m[:], in_=m[:], compare_op=ALU.not_equal, fill=1.0, base=0,
                                        pattern=[[-1, P]], channel_multiplier=1).then_inc(pool_c, 1)
            nc.gpsimd.affine_select(out=maskb[:], in_=maskb[:], compare_op=ALU.is_ge, fill=MASKED, base=0,
                                    pattern=[[-1, P]], channel_multiplier=1).then_inc(pool_c, 1)
            nc.gpsimd.affine_select(out=maskt[:], in_=maskt[:], compare_op=ALU.is_ge, fill=MASKED, base=0,
                                    pattern=[[1, P]], channel_multiplier=-1).then_inc(pool_c, 1)

            def split_wq(number):
                pool.wait_ge(wqh_done, START + number + 1)
                nc.gpsimd.tensor_tensor(wql[:], wq_raw[:], wqh[:].bitcast(F32), ALU.subtract).then_inc(wql_done, 1)

            def prologue(b):
                for u in range(2):
                    split_wq(b * UB + u + 1)

            def step(b, s, u, const, plan):
                g, tiles, steps = counts(pool, b, s, u)
                for what, arg in plan:
                    if what == "WS":
                        split_wq(g + 3)
                    if what == "R" and arg == QT:
                        divide(g)
                    if what == "ADD":
                        k = 2 * arg
                        c1 = max(0, k + 1 - QT * s) * P
                        even, odd = (prob[slot_of(steps_before(s, const) + k + i)] for i in range(2))
                        pool.wait_ge(e_done, tiles + GH * (k + 2))
                        pool.wait_ge(pv_done, steps + (k + 1))
                        nc.gpsimd.tensor_tensor(even[:, :, c1:], even[:, :, c1:], odd[:, :, c1:],
                                                ALU.add).then_inc(pair_done, 1)

            def divide(g):
                pool.wait_ge(r_done, START + QT * g)
                pool.wait_ge(at_out, START + 16 * (g - 1))
                nc.gpsimd.tensor_tensor(at_sb[:], o_sb[:], r_sb[:], ALU.mult).then_inc(at_done, 1)

            split_wq(0)
            walk(pool, prologue, step, lambda b: divide(b * UB + UB))

        @block.scalar
        def _(act):
            def split_x(b, s, j):
                n = DC * (b * NSEG + s) + j
                act.wait_ge(xt_ps, START + n + 1)
                nc.scalar.activation(xh[:, j], turned_in(s, j)[:], ACT.Copy).then_inc(xh_done, 1)

            def split_wq(number):
                act.wait_ge(wq_in, START + 16 * (number + 1))
                act.wait_ge(q_ps, START + number)
                nc.scalar.activation(wqh[:], wq_raw[:], ACT.Copy).then_inc(wqh_done, 1)

            def take_q(number, buf, old_tiles, heads=range(GH)):
                for h in heads:
                    if h == 0:
                        act.wait_ge(q_ps, START + 1 + number)
                        act.wait_ge(s_full, old_tiles)
                    nc.scalar.activation(qst[buf][0:DH, h], ps_m[h * DH:(h + 1) * DH], ACT.Copy,
                                         scale=SCALE).then_inc(qh_done, 1)

            def prologue(b):
                for j in range(DC):
                    split_x(b, 0, j)
                for u in range(2):
                    take_q(b * UB + u, u, START + b * TILES_B)
                    split_wq(b * UB + u + 1)

            def step(b, s, u, const, plan):
                g, tiles, steps = counts(act, b, s, u)
                for what, arg in plan:
                    if what == "X":
                        split_x(b, s + 1, arg)
                    if what == "WS":
                        split_wq(g + 3)
                    if what == "QE":
                        take_q(g + 2, parity(s, const + 2), tiles, [arg])
                    if what == "S":
                        k, h = arg
                        c0 = max(0, k - QT * s) * P
                        slot = slot_of(steps_before(s, const) + k)
                        bank = h % 2
                        act.wait_ge(s_full, tiles + (GH * k + h + 1))
                        if h == 0:
                            early = s == 0 and steps_before(s, const) + k < PROBS
                            act.wait_ge(sm_done, steps + (-steps_before(s, const) if early else k + 1 - PROBS))
                        nc.scalar.activation(prob[slot][:, h, c0:], ps_s[bank][:, c0:], ACT.Exp,
                                             bias=alibi_of(u, h, k - QT * s)).then_inc(e_done, 1)
                    if what == "OE":
                        act.wait_ge(sm_done, steps + ktiles(s))
                        act.wait_ge(at_done, START + g)
                        nc.scalar.activation(o_sb[:], ps_o[:], ACT.Copy).then_inc(o_copied, 1)
                        nc.scalar.activation(s_sb[:], ps_sum[:], ACT.Copy).then_inc(o_copied, 1)

            def alibi_of(u, h, dist_tiles):
                return alibi_c[:, bass.ds((u * GH + h) * (DIST0 + QT) + DIST0 + dist_tiles, 1)]

            alibi_c = alibi[:].rearrange("p h j -> p (h j)")
            act.wait_ge(vec_c, VEC_C)
            split_wq(0)
            walk(act, prologue, step, lambda b: None)

        @block.vector
        def _(dve):
            for h in range(NH):
                nc.vector.memset(slope[:, h:h + 1], slopes[h]).then_inc(vec_c, 1)
            nc.vector.memset(kexp[3 * DH:KR].bitcast(F32), 1.0).then_inc(vec_c, 1)
            dve.wait_ge(pool_c, 7)
            nc.vector.tensor_copy(dist[:], dist_i[:]).then_inc(vec_c, 1)
            nc.vector.tensor_copy(kmax[3 * DH:KR], kpos_i[3 * DH:KR]).then_inc(vec_c, 1)
            dve.wait_ge(vec_c, NH + 3)
            slope4_c = slope4[:].rearrange("p h t -> p (h t)")
            for t in range(QT):
                nc.vector.tensor_copy(slope4[:, :, t], slope[:]).then_inc(vec_c, 1)
            for h in range(NH):
                nc.vector.tensor_scalar(alibi[:, h], dist[:], slopes[h], None, ALU.mult).then_inc(vec_c, 1)
            dve.wait_ge(pe_c, 1)
            for t in range(QT):
                nc.vector.tensor_copy(slope_row[:, t * P:(t + 1) * P], ps_m[0:NH, 0:P]).then_inc(vec_c, 1)
            dve.wait_ge(wkv_in, 16)
            for r in range(3):
                nc.vector.tensor_copy(wkvh[:, :, r * DH:(r + 1) * DH], wkv_raw[:, :, 0:DH]).then_inc(vec_c, 1)
            nc.vector.tensor_copy(wkvh[:, :, 3 * DH:P], wkv_raw[:, :, DH:2 * DH]).then_inc(vec_c, 1)
            dve.wait_ge(vec_c, 2 * NH + 3 + 2 * QT + 4)
            for r in range(3):
                cols = slice(r * DH, (r + 1) * DH)
                nc.vector.tensor_tensor(wkvl[:, :, cols], wkv_raw[:, :, 0:DH], wkvh[:, :, cols].bitcast(F32),
                                        ALU.subtract).then_inc(vec_c, 1)
            nc.vector.tensor_tensor(wkvl[:, :, 3 * DH:P], wkv_raw[:, :, DH:2 * DH],
                                    wkvh[:, :, 3 * DH:P].bitcast(F32), ALU.subtract).then_inc(vec_c, 1)

            def split_x(b, s, j):
                n = DC * (b * NSEG + s) + j
                dve.wait_ge(xh_done, START + n + 1)
                nc.vector.tensor_tensor(xl[:, j], turned_in(s, j)[:], xh[:, j].bitcast(F32), ALU.subtract).then_inc(xl_done, 1)

            def take_kv(b, s):
                sg = b * NSEG + s
                cols = slice(s * QB, (s + 1) * QB)
                dve.wait_ge(kv_ps, START + sg + 1)
                if s == 0:
                    dve.wait_ge(pv_done, START + b * STEPS_B)
                nc.vector.tensor_copy(kexp[0:3 * DH, cols], ps_m[0:3 * DH]).then_inc(kv_hi, 1)
                nc.vector.tensor_copy(vt_sb[3 * DH:P], ps_m[3 * DH:P]).then_inc(kv_hi, 1)
                dve.wait_ge(kv_hi, START + 2 * (sg + 1))
                nc.vector.tensor_tensor(kexp[DH:2 * DH, cols], ps_m[DH:2 * DH], kexp[DH:2 * DH, cols].bitcast(F32),
                                        ALU.subtract).then_inc(kv_lo, 1)
                dve.wait_ge(kv_lo, START + sg + 1)
                nc.vector.tensor_copy(kmax[0:3 * DH, cols], kexp[0:3 * DH, cols].bitcast(F32)).then_inc(kv_done, 1)

            def take_v(b, s):
                sg = b * NSEG + s
                dve.wait_ge(vt_ps, START + sg + 1)
                nc.vector.tensor_copy(val[:, s * QT:(s + 1) * QT], ps_m[:, 0:QT * DH].rearrange(
                    "p (t d) -> p t d", t=QT)).then_inc(vt_done, 1)

            def take_q(g, buf, heads=range(GH)):
                for h in heads:
                    dve.wait_ge(qh_done, GH * g + (START + h + 1))
                    nc.vector.scalar_tensor_tensor(qst[buf][2 * DH:3 * DH, h], ps_m[h * DH:(h + 1) * DH], SCALE,
                                                   qst[buf][0:DH, h].bitcast(F32), ALU.mult,
                                                   ALU.subtract).then_inc(ql_done, 1)

            def maximum(tiles, i, chunk, bank):
                h, t, c, cols = chunk
                dve.wait_ge(a_full, tiles + (i + 1))
                nc.vector.tensor_reduce(mxp[:, h * QT + t, c:c + 1], ps_a[bank][:, 0:cols], AX.X,
                                        ALU.max).then_inc(a_done, 1)

            def shifts(g, tiles, s, u):
                dve.wait_ge(a_done, tiles + GH * ktiles(s))
                nc.vector.tensor_reduce(mx[:], mxp[:, :, 0:s + 1], AX.X, ALU.max).then_inc(c_max, 1)
                dve.wait_ge(c_max, START + g + 1)
                nc.vector.scalar_tensor_tensor(shift[:], slope4_c[:, bass.ds(u * (GH * QT), GH * QT)], float(QB * s),
                                               mx[:], ALU.mult, ALU.subtract).then_inc(c_vec, 1)
                dve.wait_ge(c_ps, START + g + 1)
                dve.wait_ge(c_in, START + 16 * g)
                nc.vector.tensor_copy(shift_t[:], ps_m[0:GH * QT, 0:P]).then_inc(c_out, 1)

            def divide(g, part):
                cols = slice(part * P, (part + 1) * P)
                dve.wait_ge(o_copied, START + 2 * g)
                dve.wait_ge(at_done, START + g - 1)
                nc.vector.reciprocal(r_sb[:, cols], s_sb[:, cols]).then_inc(r_done, 1)

            def prologue(b):
                for j in range(DC):
                    split_x(b, 0, j)
                take_kv(b, 0)
                take_v(b, 0)
                take_q(b * UB, 0)
                for i, chunk in enumerate(a_chunks(0)):
                    maximum(START + b * TILES_B, i, chunk, bank_of(i))
                take_q(b * UB + 1, 1)
                shifts(b * UB, START + b * TILES_B, 0, 0)

            def step(b, s, u, const, plan):
                g, tiles, steps = counts(dve, b, s, u)
                i = 0
                for what, arg in plan:
                    if what == "X":
                        split_x(b, s + 1, arg)
                    if what == "KV":
                        take_kv(b, s + 1)
                    if what == "VT":
                        take_v(b, s + 1)
                    if what == "QE":
                        take_q(g + 2, parity(s, const + 2), [arg])
                    if what == "A":
                        maximum(tiles + GH * ktiles(s), i, arg,
                                bank_of(tiles_before(*ahead(s, const, 1, const)) + i))
                        i += 1
                    if what == "CV":
                        shifts(g + 1, tiles + GH * ktiles(s), *ahead(s, u, 1, const))
                    if what == "R" and arg < QT:
                        divide(g, arg)

            def epilogue(b):
                for part in range(QT):
                    divide(b * UB + UB, part)

            walk(dve, prologue, step, epilogue)

        @block.tensor
        def _(pe):
            pe.wait_ge(pool_c, 11)
            pe.wait_ge(vec_c, NH)
            nc.tensor.transpose(ps_m[0:NH, 0:P], slope[:], ident[:]).then_inc(pe_c, 1)
            pe.wait_ge(vec_c, VEC_C)

            def turn_x(b, s, j, g):
                sg = b * NSEG + s
                if j == 0:
                    pe.wait_ge(x_in, START + 16 * (sg + 1))
                    pe.wait_ge(c_out, START + g)
                if s == 0:
                    if j == 0:
                        pe.wait_ge(a_done, START + b * TILES_B)
                    elif j > 1:
                        pe.wait_ge(xl_done, START + DC * sg + j - 1)
                elif j:
                    pe.wait_ge(xl_done, START + DC * sg + j)
                for t in range(QT):
                    last = nc.tensor.transpose(turned_in(s, j)[:, t * P:(t + 1) * P], xs[:, t, j * P:(j + 1) * P], ident[:])
                last.then_inc(xt_ps, 1)

            def three(ps, wh, wl, mh, ml, start, stop):
                nc.tensor.matmul(ps, wh, mh, start=start, stop=False)
                nc.tensor.matmul(ps, wh, ml, start=False, stop=False)
                return nc.tensor.matmul(ps, wl, mh, start=False, stop=stop)

            def project_kv(b, s):
                sg = b * NSEG + s
                pe.wait_ge(xh_done, START + DC * (sg + 1))
                pe.wait_ge(xl_done, START + DC * (sg + 1))
                for j in range(DC):
                    last = three(ps_m[:], wkvh[:, j], wkvl[:, j], xh[:, j], xl[:, j], j == 0, j == DC - 1)
                last.then_inc(kv_ps, 1)

            def turn_v(b, s):
                sg = b * NSEG + s
                pe.wait_ge(kv_done, START + sg + 1)
                pe.sem_inc(went_on, 1)
                for t in range(QT):
                    last = nc.tensor.transpose(ps_m[:, t * DH:(t + 1) * DH], vt_sb[3 * DH:P, t * P:(t + 1) * P],
                                               ident[3 * DH:P, 3 * DH:P])
                last.then_inc(vt_ps, 1)

            def project_q(g, j):
                if j == 0:
                    pe.wait_ge(wqh_done, START + g + 1)
                    pe.wait_ge(wql_done, START + g + 1)
                last = three(ps_m[:], wqh[:, j], wql[:, j], xh[:, j], xl[:, j], j == 0, j == DC - 1)
                if j == DC - 1:
                    last.then_inc(q_ps, 1)

            def scores_for_max(g, tiles, first, s, i, chunk, buf, bank):
                h, t, c, cols = chunk
                ps = ps_a[bank]
                if i == 0:
                    pe.wait_ge(stack_in, START + 32 * (g + 1))
                pe.wait_ge(a_done, tiles + (0 if first and i < 3 else i - 2))
                last = nc.tensor.matmul(ps[:, 0:cols], qst[buf][0:KR, h, t * P:(t + 1) * P],
                                        kmax[0:KR, c * QB:c * QB + cols], start=True, stop=c < s)
                if c == s:
                    last = nc.tensor.matmul(ps[:, cols - P:cols], identb[:], maskb[:], start=False, stop=True)
                last.then_inc(a_full, 1)

            def turn_shift(g):
                pe.wait_ge(c_vec, START + g + 1)
                nc.tensor.transpose(ps_m[0:GH * QT, 0:P], shift[:], ident[:]).then_inc(c_ps, 1)

            def prologue(b):
                for j in range(DC):
                    turn_x(b, 0, j, b * UB)
                project_kv(b, 0)
                turn_v(b, 0)
                pe.wait_ge(vt_done, START + b * NSEG + 1)
                for j in range(DC):
                    project_q(b * UB, j)
                for i, chunk in enumerate(a_chunks(0)):
                    scores_for_max(b * UB, START + b * TILES_B, True, 0, i, chunk, 0, bank_of(i))
                    if i == 0:
                        pe.wait_ge(ql_done, START + GH * (b * UB + 1))
                    if i % 2:
                        project_q(b * UB + 1, i // 2)
                pe.wait_ge(ql_done, START + GH * (b * UB + 2))
                turn_shift(b * UB)

            def step(b, s, u, const, plan):
                g, tiles, steps = counts(pe, b, s, u)
                buf = parity(s, const)
                i = 0
                for what, arg in plan:
                    if what == "X":
                        turn_x(b, s + 1, arg, g + 1)
                    if what == "KV":
                        project_kv(b, s + 1)
                    if what == "VT":
                        turn_v(b, s + 1)
                    if what == "Q":
                        if arg == 0 and ("VT", 0) in plan:
                            pe.wait_ge(vt_done, START + b * NSEG + s + 2)
                        elif arg == 0:
                            pe.wait_ge(c_out, START + g + 1)
                        project_q(g + 2, arg)
                    if what == "A":
                        scores_for_max(g + 1, tiles + GH * ktiles(s), False, ahead(s, 0, 1, const)[0], i, arg,
                                       parity(s, const + 1),
                                       bank_of(tiles_before(*ahead(s, const, 1, const)) + i))
                        i += 1
                    if what == "CT":
                        if ("QE", 0) in plan:
                            pe.wait_ge(ql_done, START + GH * (g + 3))
                        else:
                            pe.wait_ge(c_out, START + g + 1)
                        turn_shift(g + 1)
                    if what == "S":
                        k, h = arg
                        c0 = max(0, k - QT * s) * P
                        bank = h % 2
                        if arg == (0, 0):
                            pe.wait_ge(c_in, START + 16 * (g + 1))
                        early = s == 0 and const == 0 and GH * k + h < 2
                        pe.wait_ge(e_done, tiles + (0 if early else GH * k + h - 1))
                        diagonal = k >= QT * s
                        last = nc.tensor.matmul(ps_s[bank][:, c0:], kexp[0:KR, k * P:(k + 1) * P],
                                                qst[buf][0:KR, h, c0:], start=True, stop=not diagonal)
                        if diagonal:
                            last = nc.tensor.matmul(ps_s[bank][:, c0:c0 + P], identb[:], maskt[:], start=False,
                                                    stop=True)
                        last.then_inc(s_full, 1)
                    if what == "PV":
                        if arg == ktiles(s) - 1:
                            pe.wait_ge(e_done, tiles + GH * (arg + 1))
                        if arg == 0:
                            pe.wait_ge(o_copied, START + 2 * g)
                        over_keys(s, const, ps_o, val[:, arg], arg).then_inc(pv_done, 1)
                    if what == "SM":
                        over_keys(s, const, ps_sum, ones[:], arg).then_inc(sm_done, 1)
                    if what == "SP":
                        pe.wait_ge(pair_done, START + b * PAIRS_B + pairs_before(s, u) + arg + 1)
                        over_keys(s, const, ps_sum, ones[:], 2 * arg).then_inc(sm_done, 2)

            def over_keys(s, const, ps, weights, k):
                c0 = max(0, k - QT * s) * P
                slot = slot_of(steps_before(s, const) + k)
                for h in range(GH):
                    last = nc.tensor.matmul(ps[h * DH:(h + 1) * DH, c0:], weights, prob[slot][:, h, c0:],
                                            start=k == 0, stop=k == ktiles(s) - 1)
                return last

            walk(pe, prologue, step, lambda b: None)



def feed_forward(nc, sb, pb, sem, xt, ot, wo_v, w_v, bias, la, lb, gate_w, gate_b, att, ident):
    with ExitStack() as ctx:
        woh = sb(ctx, "woh", [P, DC, D], F32R)
        wol = sb(ctx, "wol", [P, DC, D], F32R)
        wth = sb(ctx, "wth", [P, DC, WX], F32R)
        wtl = sb(ctx, "wtl", [P, DC, WX], F32R)
        bth = sb(ctx, "bth", [RM, D], F32R)
        btl = sb(ctx, "btl", [RM, D], F32R)
        bias_b = sb(ctx, "bias_b", [P, D], F32)
        gate_bb = sb(ctx, "gate_bb", [P, NRK], F32)
        col_i = sb(ctx, "col_i", [P, RM], I32)
        col = sb(ctx, "col", [P, RM], F32)
        rank_step = sb(ctx, "rank_step", [P, NRK - 1], F32)
        at_raw = sb(ctx, "at_raw", [P, HG, P], F32)
        ath = [sb(ctx, f"ath{i}", [P, HG, P], F32R) for i in range(2)]
        atl = [sb(ctx, f"atl{i}", [P, HG, P], F32R) for i in range(2)]
        x_sb = sb(ctx, "x_sb", [P, D], F32)
        y_sb = sb(ctx, "y_sb", [P, D], F32)
        h_sb = sb(ctx, "h_sb", [P, D], F32)
        hb_sb = sb(ctx, "hb_sb", [P, D], F32)
        hth = sb(ctx, "hth", [P, DC, P], F32R)
        htl = sb(ctx, "htl", [P, DC, P], F32R)
        z_sb = [sb(ctx, f"z_sb{i}", [P, D], F32) for i in range(2)]
        stat = [sb(ctx, f"stat{i}", [P, 2, 6], F32) for i in range(2)]
        mv = [sb(ctx, f"mv{i}", [P, 2], F32) for i in range(2)]
        var = [sb(ctx, f"var{i}", [P, 1], F32) for i in range(2)]
        root = [sb(ctx, f"root{i}", [P, 1], F32) for i in range(2)]
        inv = [sb(ctx, f"inv{i}", [P, 1], F32) for i in range(2)]
        sq = [sb(ctx, f"sq{i}", [P, 1], F32) for i in range(2)]
        half = [sb(ctx, f"half{i}", [P, 1], F32) for i in range(2)]
        rstd = [sb(ctx, f"rstd{i}", [P, 1], F32) for i in range(2)]
        gate = sb(ctx, "gate", [P, NRK], F32)
        taken = sb(ctx, "taken", [P, NRK - 1], F32)
        width = sb(ctx, "width", [P, 1], F32)
        t_sb = sb(ctx, "t_sb", [P, RM], F32)
        tth = sb(ctx, "tth", [RM, P], F32R)
        ttl = sb(ctx, "ttl", [RM, P], F32R)

        ps_y = pb(ctx, "ps_y", [P, 2, 512])
        ps_t = pb(ctx, "ps_t", [P, 2, 512])
        ps_z = pb(ctx, "ps_z", [P, 3, 512])
        ps_l = pb(ctx, "ps_l", [P, 512])

        counters = []

        def counter(name):
            counters.append(sem(name))
            return counters[-1]

        went_on = sem("went_on_2")
        const_in = sem("const_in")
        f_c = sem("f_c")
        raw_buf = z_sb + [y_sb, h_sb, hb_sb]
        raw_in = [sem(f"raw_in{i}") for i in range(len(raw_buf))]
        raw_hi = sem("raw_hi")
        raw_lo = sem("raw_lo")
        raw_ps = sem("raw_ps")
        at_in = counter("at_in")
        ath_done = counter("ath_done")
        atl_done = counter("atl_done")
        x2_in = counter("x2_in")
        y_ps = counter("y_ps")
        y_done = counter("y_done")
        ln = [{n: counter(f"ln{i}_{n}") for n in ("stat", "mean", "var", "root", "inv", "sq", "half", "rstd")}
              for i in range(2)]
        h_done = counter("h_done")
        hb_done = counter("hb_done")
        t_ps = counter("t_ps")
        hth_done = counter("hth_done")
        htl_done = counter("htl_done")
        g_ps = counter("g_ps")
        g_vec = counter("g_vec")
        t_done = counter("t_done")
        l_ps = counter("l_ps")
        tth_done = counter("tth_done")
        ttl_done = counter("ttl_done")
        z_ps = counter("z_ps")
        z_done = counter("z_done")
        o_done = counter("o_done")
        o_out = [counter(f"o_out{i}") for i in range(2)]

        NZ = 3
        RAW = 2 * DC + 2
        RB = len(raw_buf)
        filled = lambda c: 16 * (c // RB + (2 if c == 2 * DC else 1))

        def walk(eng, prologue, step):
            prologue()
            with eng.Fori(0, NTT // QT - 1) as a:
                for j in range(QT):
                    step(a * QT + j, a, j, True, True)
            for j in range(QT):
                step(NTT - QT + j, NTT // QT - 1, j, j + 1 < QT, j + 2 < QT)

        def if_used_wait(eng, n, par):
            if not (isinstance(n, int) and n < 2):
                eng.wait_ge(y_ps, START + n - 1)

        def tile_after(a, j, d):
            return a + (j + d) // QT, (j + d) % QT

        def turned(ps):
            return ps[:].rearrange("p a (k r) -> p (a k) r", r=P)

        def piece(p):
            return slice(p * WCH, (p + 1) * WCH)

        last_piece = D - (NZ - 1) * WCH
        with nc.Block() as start:
            @start.sync
            def _(sp):
                for c in counters:
                    sp.sem_inc(c, START)

        block = ctx.enter_context(nc.Block())

        @block.sync
        def _(sp):
            sp.dma_start(bias_b[:], bias.partition_broadcast(P)).then_inc(const_in, 16)
            sp.dma_start(gate_bb[:], gate_b.partition_broadcast(P)).then_inc(const_in, 16)
            for c in range(RAW):
                if c >= RB:
                    sp.wait_ge(raw_lo, c - RB + 1)
                raw = raw_buf[c % RB]
                if c < DC:
                    sp.dma_start(raw[:], wo_v[c]).then_inc(raw_in[c % RB], 16)
                elif c < 2 * DC:
                    sp.dma_start(raw[:], w_v[c - DC]).then_inc(raw_in[c % RB], 16)
                elif c == 2 * DC:
                    sp.dma_start(raw[0:RM], la).then_inc(raw_in[c % RB], 16)
                    sp.dma_start(raw[RM:RM + NRK], gate_w).then_inc(raw_in[c % RB], 16)
                else:
                    sp.dma_start(raw[:, 0:DC * RM].rearrange("p (o r) -> p o r", o=DC),
                                 lb.rearrange("(o p) r -> p o r", p=P)).then_inc(raw_in[c % RB], 16)

            def load_at(n, a, t):
                sp.wait_ge(ath_done, START + n)
                sp.wait_ge(atl_done, START + n)
                sp.dma_start(at_raw[:], att_tiles[a, t]).then_inc(at_in, 16)

            def load_x(n):
                sp.wait_ge(y_done, START + n)
                sp.dma_start(x_sb[:], xt[n]).then_inc(x2_in, 16)

            att_tiles = att.rearrange("(a g) t p q -> a t p g q", g=HG)

            def prologue():
                load_at(0, 0, 0)
                load_x(0)
                load_at(1, 0, 1)

            def step(n, a, j, has_next, has_after):
                if has_next:
                    load_x(n + 1)
                if has_after:
                    load_at(n + 2, *tile_after(a, j, 2))
                sp.wait_ge(o_done, START + n + 1)
                sp.dma_start(ot[n], z_sb[j % 2][:]).then_inc(o_out[j % 2], 16)

            walk(sp, prologue, step)
            for par in range(2):
                sp.wait_ge(o_out[par], START + 16 * NTT // 2)

        @block.gpsimd
        def _(pool):
            nc.gpsimd.iota(col_i[:], [[1, RM]], base=-RANKS[0], channel_multiplier=0).then_inc(f_c, 1)
            for r in range(NRK - 1):
                nc.gpsimd.memset(rank_step[:, r:r + 1], float(RANKS[r + 1] - RANKS[r])).then_inc(f_c, 1)
            pool.wait_ge(const_in, 32)

            def add_bias(n):
                pool.wait_ge(h_done, START + n + 1)
                pool.wait_ge(z_done, START + 2 * n)
                nc.gpsimd.tensor_tensor(hb_sb[:], h_sb[:], bias_b[:], ALU.add).then_inc(hb_done, 1)

            walk(pool, lambda: add_bias(0),
                 lambda n, a, j, has_next, has_after: add_bias(n + 1) if has_next else None)

        @block.scalar
        def _(act):
            for c in range(RAW):
                if c < DC:
                    act.wait_ge(raw_in[c % RB], filled(c))
                    nc.scalar.activation(woh[:, c], raw_buf[c % RB][:], ACT.Copy).then_inc(raw_hi, 1)
                else:
                    act.wait_ge(raw_ps, c - DC + 1)
                    src = turned(ps_t if c % 2 else ps_y)
                    if c < 2 * DC:
                        o = c - DC
                        nc.scalar.activation(wth[:, :, o * P:(o + 1) * P], src, ACT.Copy).then_inc(raw_hi, 1)
                    elif c == 2 * DC:
                        nc.scalar.activation(wth[:, :, D:WX], src[:, :, 0:RM + NRK], ACT.Copy).then_inc(raw_hi, 1)
                    else:
                        nc.scalar.activation(bth[:].rearrange("r (o p) -> r o p", p=P), src[0:RM],
                                             ACT.Copy).then_inc(raw_hi, 1)

            def split_at(n, par):
                act.wait_ge(at_in, START + 16 * (n + 1))
                if_used_wait(act, n, par)
                nc.scalar.activation(ath[par][:], at_raw[:], ACT.Copy).then_inc(ath_done, 1)

            def take_root(i, n):
                act.wait_ge(ln[i]["var"], START + n + 1)
                nc.scalar.activation(root[i][:], var[i][:], ACT.Sqrt).then_inc(ln[i]["root"], 1)

            def prologue():
                split_at(0, 0)
                split_at(1, 1)
                take_root(0, 0)

            def step(n, a, j, has_next, has_after):
                act.wait_ge(t_ps, START + n + 1)
                nc.scalar.activation(hth[:], turned(ps_t), ACT.Copy).then_inc(hth_done, 1)
                if has_next:
                    take_root(0, n + 1)
                act.wait_ge(l_ps, START + n + 1)
                nc.scalar.activation(tth[:], ps_l[0:RM, 0:P], ACT.Copy).then_inc(tth_done, 1)
                if has_after:
                    split_at(n + 2, j % 2)
                take_root(1, n)

            walk(act, prologue, step)

        @block.vector
        def _(dve):
            for c in range(RAW):
                dve.wait_ge(raw_hi, c + 1)
                src = turned(ps_t if c % 2 else ps_y)
                if c < DC:
                    nc.vector.tensor_tensor(wol[:, c], raw_buf[c % RB][:], woh[:, c].bitcast(F32),
                                            ALU.subtract).then_inc(raw_lo, 1)
                elif c < 2 * DC:
                    cols = slice((c - DC) * P, (c - DC + 1) * P)
                    nc.vector.tensor_tensor(wtl[:, :, cols], src, wth[:, :, cols].bitcast(F32),
                                            ALU.subtract).then_inc(raw_lo, 1)
                elif c == 2 * DC:
                    nc.vector.tensor_tensor(wtl[:, :, D:WX], src[:, :, 0:RM + NRK], wth[:, :, D:WX].bitcast(F32),
                                            ALU.subtract).then_inc(raw_lo, 1)
                else:
                    nc.vector.tensor_tensor(btl[:].rearrange("r (o p) -> r o p", p=P), src[0:RM],
                                            bth[:].rearrange("r (o p) -> r o p", p=P).bitcast(F32),
                                            ALU.subtract).then_inc(raw_lo, 1)
            dve.wait_ge(f_c, NRK)
            nc.vector.tensor_copy(col[:], col_i[:]).then_inc(f_c, 1)
            dve.wait_ge(f_c, NRK + 1)
            dve.wait_ge(const_in, 32)

            def split_at(n, par):
                dve.wait_ge(ath_done, START + n + 1)
                if_used_wait(dve, n, par)
                nc.vector.tensor_tensor(atl[par][:], at_raw[:], ath[par][:].bitcast(F32),
                                        ALU.subtract).then_inc(atl_done, 1)

            def norm(i, n, src, dst, done):
                s = ln[i]
                for k in range(2):
                    nc.vector.bn_stats(stat[i][:, k], src[:, k * 512:(k + 1) * 512]).then_inc(s["stat"], 1)
                dve.wait_ge(s["stat"], START + 2 * (n + 1))
                dve.sem_inc(went_on, 1)
                nc.vector.bn_aggr(mv[i][:], stat[i][:].rearrange("p a k -> p (a k)")).then_inc(s["mean"], 1)
                dve.wait_ge(s["mean"], START + n + 1)
                nc.vector.tensor_scalar(var[i][:], mv[i][:, 1:2], EPS, None, ALU.add).then_inc(s["var"], 1)
                dve.wait_ge(s["root"], START + n + 1)
                nc.vector.reciprocal(inv[i][:], root[i][:]).then_inc(s["inv"], 1)
                dve.wait_ge(s["inv"], START + n + 1)
                nc.vector.tensor_tensor(sq[i][:], inv[i][:], inv[i][:], ALU.mult).then_inc(s["sq"], 1)
                dve.wait_ge(s["sq"], START + n + 1)
                nc.vector.scalar_tensor_tensor(half[i][:], sq[i][:], -0.5, var[i][:], ALU.mult,
                                               ALU.mult).then_inc(s["half"], 1)
                dve.wait_ge(s["half"], START + n + 1)
                nc.vector.scalar_tensor_tensor(rstd[i][:], half[i][:], 1.5, inv[i][:], ALU.add,
                                               ALU.mult).then_inc(s["rstd"], 1)
                dve.wait_ge(s["rstd"], START + n + 1)
                nc.vector.tensor_scalar(dst, src, mv[i][:, 0:1], rstd[i][:, 0:1], ALU.subtract,
                                        ALU.mult).then_inc(done, 1)

            def first_norm(n):
                dve.wait_ge(y_ps, START + n + 1)
                dve.wait_ge(x2_in, START + 16 * (n + 1))
                nc.vector.tensor_tensor(y_sb[:], ps_y[:].rearrange("p a n -> p (a n)"), x_sb[:],
                                        ALU.add).then_inc(y_done, 1)
                dve.wait_ge(y_done, START + n + 1)
                dve.wait_ge(t_ps, START + n)
                dve.wait_ge(hb_done, START + n)
                norm(0, n, y_sb[:], h_sb[:], h_done)

            def choose(n):
                dve.wait_ge(g_ps, START + n + 1)
                g = ps_z[:, NZ - 1, last_piece + RM:WCH]
                nc.vector.tensor_tensor(gate[:], g, gate_bb[:], ALU.add).then_inc(g_vec, 1)
                for r in range(1, NRK):
                    dve.wait_ge(g_vec, START + (NRK + 1) * n + r)
                    nc.vector.tensor_tensor(gate[:, r:r + 1], gate[:, r - 1:r], gate[:, r:r + 1],
                                            ALU.max).then_inc(g_vec, 1)
                dve.wait_ge(g_vec, START + (NRK + 1) * n + NRK)
                nc.vector.scalar_tensor_tensor(taken[:], gate[:, 0:NRK - 1], gate[:, NRK - 1:NRK], rank_step[:],
                                               ALU.is_lt, ALU.mult, accum_out=width[:]).then_inc(g_vec, 1)
                dve.wait_ge(g_vec, START + (NRK + 1) * (n + 1))
                nc.vector.scalar_tensor_tensor(t_sb[:], col[:], width[:, 0:1],
                                               ps_z[:, NZ - 1, last_piece:last_piece + RM],
                                               ALU.is_lt, ALU.mult).then_inc(t_done, 1)
                dve.wait_ge(tth_done, START + n + 1)
                nc.vector.tensor_tensor(ttl[:], ps_l[0:RM, 0:P], tth[:].bitcast(F32),
                                        ALU.subtract).then_inc(ttl_done, 1)

            def second_norm(n, j, stored):
                z = z_sb[j % 2]
                dve.wait_ge(z_ps, START + n + 1)
                dve.wait_ge(hb_done, START + n + 1)
                dve.wait_ge(o_out[j % 2], START + 16 * stored)
                cut = (NZ - 1) * WCH
                nc.vector.tensor_tensor(z[:, 0:cut].rearrange("p (a n) -> p a n", n=WCH), ps_z[:, 0:NZ - 1, 0:WCH],
                                        hb_sb[:, 0:cut].rearrange("p (a n) -> p a n", n=WCH),
                                        ALU.add).then_inc(z_done, 1)
                nc.vector.tensor_tensor(z[:, cut:D], ps_z[:, NZ - 1, 0:last_piece], hb_sb[:, cut:D],
                                        ALU.add).then_inc(z_done, 1)
                dve.wait_ge(z_done, START + 2 * (n + 1))
                norm(1, n, z[:], z[:], o_done)

            def prologue():
                split_at(0, 0)
                split_at(1, 1)
                first_norm(0)

            def step(n, a, j, has_next, has_after):
                dve.wait_ge(hth_done, START + n + 1)
                nc.vector.tensor_tensor(htl[:], turned(ps_t), hth[:].bitcast(F32), ALU.subtract).then_inc(htl_done, 1)
                if has_next:
                    first_norm(n + 1)
                choose(n)
                if has_after:
                    split_at(n + 2, j % 2)
                second_norm(n, j, a * (QT // 2) + j // 2)

            walk(dve, prologue, step)

        @block.tensor
        def _(pe):
            for c in range(DC, RAW):
                pe.wait_ge(raw_in[c % RB], filled(c))
                pe.wait_ge(raw_lo, c - 1)
                raw, ps = raw_buf[c % RB], ps_t if c % 2 else ps_y
                for k in range(DC):
                    dst = ps[:, k // QT, (k % QT) * P:(k % QT + 1) * P]
                    if c < 2 * DC:
                        last = nc.tensor.transpose(dst, raw[:, k * P:(k + 1) * P], ident[:])
                    elif c == 2 * DC:
                        last = nc.tensor.transpose(dst[:, 0:RM + NRK], raw[0:RM + NRK, k * P:(k + 1) * P],
                                                   ident[0:RM + NRK, 0:RM + NRK])
                    else:
                        last = nc.tensor.transpose(dst[0:RM], raw[:, k * RM:(k + 1) * RM], ident[:])
                last.then_inc(raw_ps, 1)
            pe.wait_ge(raw_lo, RAW)

            def first_product(n, par):
                pe.wait_ge(ath_done, START + n + 1)
                pe.wait_ge(atl_done, START + n + 1)
                pe.wait_ge(y_done, START + n)
                for half_no in range(2):
                    cols = slice(half_no * 512, (half_no + 1) * 512)
                    ps = ps_y[:, half_no]
                    for c in range(HG):
                        first, end = c == 0, c == HG - 1
                        nc.tensor.matmul(ps, ath[par][:, c], woh[:, c, cols], start=first, stop=False)
                        nc.tensor.matmul(ps, ath[par][:, c], wol[:, c, cols], start=False, stop=False)
                        last = nc.tensor.matmul(ps, atl[par][:, c], woh[:, c, cols], start=False, stop=end)
                last.then_inc(y_ps, 1)

            def second_product(n, p):
                ps = ps_z[:, p, 0:WCH]
                for c in range(DC):
                    nc.tensor.matmul(ps, hth[:, c], wth[:, c, piece(p)], start=c == 0, stop=False,
                                     skip_group_check=True)
                    nc.tensor.matmul(ps, hth[:, c], wtl[:, c, piece(p)], start=False, stop=False,
                                     skip_group_check=True)
                    last = nc.tensor.matmul(ps, htl[:, c], wth[:, c, piece(p)], start=False, stop=False,
                                            skip_group_check=True)
                return last

            def step(n, a, j, has_next, has_after):
                pe.wait_ge(h_done, START + n + 1)
                pe.wait_ge(htl_done, START + n)
                for k in range(DC):
                    last = nc.tensor.transpose(ps_t[:, k // QT, (k % QT) * P:(k % QT + 1) * P],
                                               h_sb[:, k * P:(k + 1) * P], ident[:])
                last.then_inc(t_ps, 1)
                if has_next:
                    first_product(n + 1, (j + 1) % 2)
                pe.wait_ge(hth_done, START + n + 1)
                pe.wait_ge(htl_done, START + n + 1)
                pe.wait_ge(z_done, START + 2 * n)
                second_product(n, NZ - 1).then_inc(g_ps, 1)
                second_product(n, 0)
                pe.wait_ge(t_done, START + n + 1)
                pe.wait_ge(ttl_done, START + n)
                pe.sem_inc(went_on, 1)
                nc.tensor.transpose(ps_l[0:RM, 0:P], t_sb[:], ident[:]).then_inc(l_ps, 1)
                second_product(n, 1)
                pe.wait_ge(tth_done, START + n + 1)
                pe.wait_ge(ttl_done, START + n + 1)
                for p in range(NZ):
                    cols = slice(p * WCH, min(D, (p + 1) * WCH))
                    ps = ps_z[:, p, 0:cols.stop - cols.start]
                    nc.tensor.matmul(ps, tth[:], bth[:, cols], start=False, stop=False, skip_group_check=True)
                    nc.tensor.matmul(ps, tth[:], btl[:, cols], start=False, stop=False, skip_group_check=True)
                    last = nc.tensor.matmul(ps, ttl[:], bth[:, cols], start=False, stop=True,
                                            skip_group_check=True)
                last.then_inc(z_ps, 1)

            walk(pe, lambda: first_product(0, 0), step)


_INS = ["L0_attn_hidden_states", "L0_attn_Wq", "L0_attn_Wkv", "L0_attn_Wo", "L0_ffn_W", "L0_ffn_b", "L0_ffn_A",
        "L0_ffn_B", "L0_ffn_gate_w", "L0_ffn_gate_b"]


def kernel(**inputs):
    import concourse.bacc as bacc
    from concourse.bass_utils import run_bass_kernel_spmd

    nc = bacc.Bacc("TRN2", target_bir_lowering=False, num_devices=1)
    arrays, args = {}, []
    for name in _INS:
        a = np.ascontiguousarray(inputs[name])
        arrays[f"in_{name}"] = a
        args.append(nc.dram_tensor(f"in_{name}", a.shape, mybir.dt.from_np(a.dtype), kind="ExternalInput").ap())
    out = nc.dram_tensor("out", (B, T, D), F32, kind="ExternalOutput").ap()
    program(nc, *args, out)
    r = run_bass_kernel_spmd(nc, [arrays], core_ids=[0])
    return r.results[0]["out"]
```
